# Optimizing a Trainium2 kernel written in Bass

```python
import numpy as np
import jax
import jax.numpy as jnp

def _softmax(x, axis=-1):
    return jax.nn.softmax(x, axis=axis)

def _gelu(x):
    return jax.nn.gelu(x, approximate=True)

def _silu(x):
    return jax.nn.silu(x)

def _sigmoid(x):
    return jax.nn.sigmoid(x)

def _layernorm(x, axis=-1, eps=1e-05):
    m = jnp.mean(x, axis=axis, keepdims=True)
    v = jnp.var(x, axis=axis, keepdims=True)
    return (x - m) / jnp.sqrt(v + eps)

def _scatter_add(tgt, idx, src, axis=0):
    return tgt.at[idx].add(src)

def _segment_sum(src, seg, n):
    return jax.ops.segment_sum(src, seg, n)
kernel_name = 'mk_xattn_ffn_d2_seqx_r8_f33666'

def setup_inputs(seed: int=0):
    np.random.seed(seed)
    _w = jnp.asarray

    def _rec_inputs():
        import jax
        import jax.numpy as jnp
        _rk = jax.random.key(seed)
        x = -0.0002928 + 1 * jax.random.normal(jax.random.fold_in(_rk, 1), (32, 56, 128), jnp.float32)
        _lenS = 56 - jax.random.randint(jax.random.fold_in(_rk, 7), (32,), 0, max(1, 56 // 4) + 1, jnp.int32)
        _lenS2 = 1500 - jax.random.randint(jax.random.fold_in(_rk, 8), (32,), 0, max(1, 1500 // 4) + 1, jnp.int32)
        _ctx_1024P = jax.random.normal(jax.random.fold_in(_rk, 11), (32, 16, 128), jnp.float32)
        _ctx_1024c = jax.random.dirichlet(jax.random.fold_in(_rk, 511), 0.3 * jnp.ones((16,), jnp.float32), (32, 1500))
        _ctx_1024t = jnp.einsum('bsk,bkd->bsd', _ctx_1024c, _ctx_1024P)
        _ctx_1024t = _ctx_1024t * jax.lax.rsqrt(jnp.mean(jnp.square(_ctx_1024t)) + 1e-12) * 0.953939
        ctx_1024 = -1.39393e-06 + 0.999914 * (_ctx_1024t + 0.3 * jax.random.normal(jax.random.fold_in(_rk, 611), (32, 1500, 128), jnp.float32))
        _validS = jnp.arange(56)[None, :] < _lenS[:, None]
        _validS2 = jnp.arange(1500)[None, :] < _lenS2[:, None]
        _causal = jnp.tril(jnp.ones((56, 56), dtype=bool))
        mask_BxS2_ik0 = jnp.where(jnp.broadcast_to(_validS2[:, :], (32, 1500)), 0, 1).astype(jnp.int32)
        return (x, ctx_1024, mask_BxS2_ik0)
    x, ctx_1024, mask_BxS2_ik0 = _rec_inputs()

    def _L0_xattn_setup():
        import jax, jax.numpy as jnp
        import numpy as np
        N_HEADS = 16
        D_IN = 128
        D_K = 64
        D_V_HEAD = 128 // N_HEADS
        key = jax.random.key(seed)
        k1, k2, k3, k4, k5 = jax.random.split(key, 5)
        B, LQ, LK = (2, 256, 256)
        s = 1.0 / np.sqrt(D_IN)
        return {'input_q': jax.random.normal(k1, (B, LQ, D_IN), dtype=jnp.float32), 'input_k': jax.random.normal(k2, (B, LK, D_IN), dtype=jnp.float32), 'wq': jax.random.uniform(k3, (D_IN, D_K * N_HEADS), jnp.float32, -s, s), 'wk': jax.random.uniform(k4, (D_IN, D_K * N_HEADS), jnp.float32, -s, s), 'wv': jax.random.uniform(k5, (D_IN, D_V_HEAD * N_HEADS), jnp.float32, -s, s)}
    _L0_xattn_all = _L0_xattn_setup()
    _L0_xattn_in = {k: v for k, v in _L0_xattn_all.items() if k in ('wq', 'wk', 'wv')}
    del _L0_xattn_all

    def _L0_ffn_setup():
        import jax, jax.numpy as jnp
        import numpy as np
        B, S, D, E, F = (2, 256, 128, 8, 512)
        key = jax.random.key(seed)
        ks = jax.random.split(key, 4)
        return {'hidden_states': jax.random.normal(ks[0], (B, S, D), dtype=jnp.float32), 'Wr': jax.random.normal(ks[1], (D, E), dtype=jnp.float32) * (1.0 / np.sqrt(D)), 'W1': jax.random.normal(ks[2], (E, D, F), dtype=jnp.float32) * (1.0 / np.sqrt(D)), 'b1': jnp.zeros((E, F), dtype=jnp.float32), 'W2': jax.random.normal(ks[3], (E, F, D), dtype=jnp.float32) * (1.0 / np.sqrt(F)), 'b2': jnp.zeros((E, D), dtype=jnp.float32)}
    _L0_ffn_all = _L0_ffn_setup()
    _L0_ffn_in = {k: v for k, v in _L0_ffn_all.items() if k in ('Wr', 'W1', 'b1', 'W2', 'b2')}
    del _L0_ffn_all

    def _L1_xattn_setup():
        import jax, jax.numpy as jnp
        import numpy as np
        B, SQ, SKV, D, H = (2, 256, 256, 128, 16)
        W = D // H

        def _heads(x):
            b, s, _ = x.shape
            return x.reshape(b, s, H, W).transpose(0, 2, 1, 3)
        key = jax.random.key(seed)
        ks = jax.random.split(key, 10)
        s = 1.0 / np.sqrt(D)
        return {'x_q': jax.random.normal(ks[0], (B, SQ, D), jnp.float32), 'x_k': jax.random.normal(ks[1], (B, SKV, D), jnp.float32), 'x_v': jax.random.normal(ks[2], (B, SKV, D), jnp.float32), 'mask': jax.random.randint(ks[3], (B, SKV), 0, 2, jnp.int32), 'Wq': jax.random.normal(ks[4], (D, D), jnp.float32) * s, 'bq': jnp.zeros((D,), jnp.float32), 'Wk': jax.random.normal(ks[5], (D, D), jnp.float32) * s, 'bk': jnp.zeros((D,), jnp.float32), 'Wv': jax.random.normal(ks[6], (D, D), jnp.float32) * s, 'bv': jnp.zeros((D,), jnp.float32)}
    _L1_xattn_all = _L1_xattn_setup()
    _L1_xattn_in = {k: v for k, v in _L1_xattn_all.items() if k in ('Wq', 'bq', 'Wk', 'bk', 'Wv', 'bv')}
    del _L1_xattn_all

    def _L1_ffn_setup():
        import jax, jax.numpy as jnp
        import numpy as np
        import math
        N_EXP = 8
        TOP_K = 2
        CAPACITY_FACTOR = 1.25

        def _capacity(num_tokens):
            cap = math.floor(TOP_K * CAPACITY_FACTOR * num_tokens / N_EXP)
            cap += cap % 2
            return int(cap)
        key = jax.random.key(seed)
        k1, k2, k3, k4 = jax.random.split(key, 4)
        B, C, d = (4, 128, 128)
        x = jax.random.normal(k1, (B, C, d), dtype=jnp.float32)
        w_g = jax.random.normal(k2, (d, N_EXP), dtype=jnp.float32) * 0.02
        c_fc = jax.random.normal(k3, (N_EXP, d, 4 * d), dtype=jnp.float32) * 0.02
        c_proj = jax.random.normal(k4, (N_EXP, 4 * d, d), dtype=jnp.float32) * 0.02
        return {'x': x, 'w_g': w_g, 'c_fc': c_fc, 'c_proj': c_proj}
    _L1_ffn_all = _L1_ffn_setup()
    _L1_ffn_in = {k: v for k, v in _L1_ffn_all.items() if k in ('w_g', 'c_fc', 'c_proj')}
    del _L1_ffn_all
    return {'x': x, 'ctx_1024': ctx_1024, 'mask_BxS2_ik0': mask_BxS2_ik0, 'L0_xattn_wq': _L0_xattn_in['wq'], 'L0_xattn_wk': _L0_xattn_in['wk'], 'L0_xattn_wv': _L0_xattn_in['wv'], 'L0_ffn_Wr': _L0_ffn_in['Wr'], 'L0_ffn_W1': _L0_ffn_in['W1'], 'L0_ffn_b1': _L0_ffn_in['b1'], 'L0_ffn_W2': _L0_ffn_in['W2'], 'L0_ffn_b2': _L0_ffn_in['b2'], 'L1_xattn_Wq': _L1_xattn_in['Wq'], 'L1_xattn_bq': _L1_xattn_in['bq'], 'L1_xattn_Wk': _L1_xattn_in['Wk'], 'L1_xattn_bk': _L1_xattn_in['bk'], 'L1_xattn_Wv': _L1_xattn_in['Wv'], 'L1_xattn_bv': _L1_xattn_in['bv'], 'L1_ffn_w_g': _L1_ffn_in['w_g'], 'L1_ffn_c_fc': _L1_ffn_in['c_fc'], 'L1_ffn_c_proj': _L1_ffn_in['c_proj']}

def reference(x, ctx_1024, mask_BxS2_ik0, L0_xattn_wq, L0_xattn_wk, L0_xattn_wv, L0_ffn_Wr, L0_ffn_W1, L0_ffn_b1, L0_ffn_W2, L0_ffn_b2, L1_xattn_Wq, L1_xattn_bq, L1_xattn_Wk, L1_xattn_bk, L1_xattn_Wv, L1_xattn_bv, L1_ffn_w_g, L1_ffn_c_fc, L1_ffn_c_proj):
    import jax
    import jax.numpy as jnp

    def _L0_xattn_ref(input_q, input_k, wq, wk, wv):
        import jax, jax.numpy as jnp
        import numpy as np
        N_HEADS = 16
        D_IN = 128
        D_K = 64
        D_V_HEAD = 128 // N_HEADS
        B, LQ, _ = input_q.shape
        _, LK, _ = input_k.shape
        q = (input_q @ wq).reshape(B, LQ, N_HEADS, D_K).transpose(0, 2, 1, 3)
        k = (input_k @ wk).reshape(B, LK, N_HEADS, D_K).transpose(0, 2, 1, 3)
        v = (input_k @ wv).reshape(B, LK, N_HEADS, D_V_HEAD).transpose(0, 2, 1, 3)
        attn = jnp.einsum('bhqd,bhkd->bhqk', q, k) / jnp.sqrt(jnp.float32(D_K))
        attn = jax.nn.softmax(attn, axis=-1)
        out = jnp.einsum('bhqk,bhkd->bhqd', attn, v)
        return out.transpose(0, 2, 1, 3).reshape(B, LQ, D_V_HEAD * N_HEADS)

    def _L0_ffn_ref(hidden_states, Wr, W1, b1, W2, b2):
        import jax, jax.numpy as jnp
        import numpy as np
        B, S, D, E, F = (2, 256, 128, 8, 512)
        b, s, d = hidden_states.shape
        e = Wr.shape[1]
        x = hidden_states.reshape(b * s, d)
        router_logits = x @ Wr
        router_probs = jax.nn.softmax(router_logits, axis=-1)
        expert_idx = jnp.argmax(router_probs, axis=-1)
        p_max = jnp.max(router_probs, axis=-1, keepdims=True)

        def expert_mlp(w1, bb1, w2, bb2):
            h = jax.nn.gelu(x @ w1 + bb1, approximate=False)
            return h @ w2 + bb2
        outs = jax.vmap(expert_mlp)(W1, b1, W2, b2)
        onehot = jax.nn.one_hot(expert_idx, e, dtype=x.dtype)
        next_states = jnp.einsum('te,etd->td', onehot, outs)
        out = p_max * next_states
        return out.reshape(b, s, d)

    def _L1_xattn_ref(x_q, x_k, x_v, mask, Wq, bq, Wk, bk, Wv, bv):
        import jax, jax.numpy as jnp
        import numpy as np
        B, SQ, SKV, D, H = (2, 256, 256, 128, 16)
        W = D // H

        def _heads(x):
            b, s, _ = x.shape
            return x.reshape(b, s, H, W).transpose(0, 2, 1, 3)
        q = _heads(x_q @ Wq.T + bq)
        k = _heads(x_k @ Wk.T + bk)
        v = _heads(x_v @ Wv.T + bv)
        scores = jnp.einsum('bhqw,bhkw->bhqk', q, k) / np.sqrt(W).astype(np.float32)
        m = mask[:, None, None, :].astype(scores.dtype)
        scores = scores - 10000.0 * (1.0 - m)
        p = jax.nn.softmax(scores, axis=-1)
        h = jnp.einsum('bhqk,bhkw->bhqw', p, v)
        return h.transpose(0, 2, 1, 3).reshape(x_q.shape[0], x_q.shape[1], D)

    def _L1_ffn_ref(x, w_g, c_fc, c_proj):
        import jax, jax.numpy as jnp
        import numpy as np
        import math
        N_EXP = 8
        TOP_K = 2
        CAPACITY_FACTOR = 1.25

        def _capacity(num_tokens):
            cap = math.floor(TOP_K * CAPACITY_FACTOR * num_tokens / N_EXP)
            cap += cap % 2
            return int(cap)
        B, C, d = x.shape
        T = B * C
        cap = _capacity(T)
        xt = x.reshape(T, d)
        logits = xt @ w_g
        top_v, top_i = jax.lax.top_k(logits, TOP_K)
        full = jnp.full_like(logits, -jnp.inf)
        full = full.at[jnp.arange(T)[:, None], top_i].set(top_v)
        probs = jax.nn.softmax(full, axis=-1)
        exp_mask = jax.nn.one_hot(top_i, N_EXP, dtype=jnp.int32)
        exp_mask = jnp.transpose(exp_mask, (1, 0, 2))
        exp_rank = jnp.cumsum(exp_mask.reshape(TOP_K * T, N_EXP), axis=0) - 1
        exp_rank = exp_rank.reshape(TOP_K, T, N_EXP)
        exp_mask = exp_mask * (exp_rank < cap).astype(jnp.int32)
        exp_rank = jnp.sum(exp_mask * exp_rank, axis=-1)
        exp_weights = exp_mask.astype(x.dtype) * probs[None]
        rank_oh = jax.nn.one_hot(exp_rank, cap, dtype=x.dtype)
        cb_weight = jnp.einsum('kte,ktc->tec', exp_weights, rank_oh)
        sec_mask = (cb_weight != 0).astype(x.dtype)
        exp_batches = jnp.einsum('tec,td->ecd', sec_mask, xt)
        h = jax.nn.gelu(jnp.einsum('ecd,edf->ecf', exp_batches, c_fc), approximate=False)
        exp_out = jnp.einsum('ecf,efd->ecd', h, c_proj)
        out = cb_weight.reshape(T, N_EXP * cap) @ exp_out.reshape(N_EXP * cap, d)
        return out.reshape(B, C, d)
    x = x + _L0_xattn_ref(_layernorm(x, axis=-1), ctx_1024, L0_xattn_wq, L0_xattn_wk, L0_xattn_wv)
    x = x + _L0_ffn_ref(_layernorm(x, axis=-1), L0_ffn_Wr, L0_ffn_W1, L0_ffn_b1, L0_ffn_W2, L0_ffn_b2)
    x = x + _L1_xattn_ref(_layernorm(x, axis=-1), ctx_1024, ctx_1024, mask_BxS2_ik0, L1_xattn_Wq, L1_xattn_bq, L1_xattn_Wk, L1_xattn_bk, L1_xattn_Wv, L1_xattn_bv)
    x = x + _L1_ffn_ref(_layernorm(x, axis=-1), L1_ffn_w_g, L1_ffn_c_fc, L1_ffn_c_proj)
    return x

_drawn_inputs = setup_inputs


def setup_inputs(seed=0):
    import zlib

    import numpy as np

    out = dict(_drawn_inputs(seed))
    spreads = {'L0_ffn_b1': (0.0, 0.352),
     'L0_ffn_b2': (0.0, 0.1),
     'L1_xattn_bq': (0.0, 0.408),
     'L1_xattn_bk': (0.0, 0.8),
     'L1_xattn_bv': (0.0, 0.1)}
    factors = {}
    for name, (base, spread) in spreads.items():
        noise = np.random.default_rng([zlib.crc32(name.encode()), seed]).standard_normal(out[name].shape)
        drawn = base * np.exp(spread * noise) if base else spread * noise
        out[name] = jnp.asarray(drawn.astype(out[name].dtype))
    for name, factor in factors.items():
        out[name] = (out[name] * factor).astype(out[name].dtype)
    return out
```

```python
from contextlib import ExitStack

import numpy as np

import concourse.bass as bass
from concourse import mybir

F32 = mybir.dt.float32
F16 = mybir.dt.float16
I32 = mybir.dt.int32
ALU = mybir.AluOpType
ACT = mybir.ActivationFunctionType
AX = mybir.AxisListType

S, D = 56, 128
NK, CH = 1500, 12
CK = NK // CH
H = 16
DK0 = 64
W = D // H
NP = H // 2
PR = 2 * S
NG = 4
GW = D // NG
COLS = H * S
HB = COLS // 2
BANK = 512
KB = 500
NKB = NK // KB
PB = 64
E, FF = 8, 512
NF = FF // 128
SHIFT = 96
NSH = 1 + NP
TOPM = 10000.0
PROB = 6
EPS = 1e-5

def spread(counts):
    at, out = 0, []
    for n in counts:
        out.append([f"M{m}" for m in range(at, at + n)])
        at += n
    assert at == NP * NKB
    return out


UNITS0 = [["T0", "T1"], ["T2", "Q0"], ["Q1", "V0"], ["V1", "V2"]] + spread([3, 3, 3, 4, 4, 4, 3]) + [["R"]]
UNITS1 = [["T0", "T1", "T2"], ["K0", "K1", "K2"], ["Q0", "V0", "V1"], ["V2", "V3"]] + spread([3, 3, 3, 4, 4, 4, 3]) + [["R"]]
ACT_READS = ["TQ", "TKV"]
ACT_RELEASES = ["", "V"]
PV_AT = [[-2], [-1], [], [], [0], [1, 2], [3, 4], [5], [6], [7], [8], [9]]
OUT_AT = 3


class Step:

    def __init__(self, j, c):
        self.j, self.c = j, c

    def value(self, per, k, back=0):
        c = (self.c - back) * per + k
        return c if self.j is None else self.j * (2 * per) + c


class Signal:

    def __init__(self, sem, per, first):
        self.sem, self.per, self.first = sem, per, first

    def wait(self, eng, st, k, back=0):
        v = st.value(self.per, k, back + self.first)
        if st.j is not None or v > 0:
            eng.wait_ge(self.sem, v)


def program(nc, B, args, out):
    (x, ctx_d, mask, wqT, wkT, wv, wr0, w1, b1, w2, b2rep, wq1T, bqr, wk1T, bk, wv1T, bv, wg, fc,
     proj, ident_d, negid_d, hmask_d, sel0_d, sel1_d, selte_d, tri_d, real_d, eidx_d) = args
    NT = B // 2
    TOK = NT * 128
    G = B // 8
    T = B * S
    cap = int(2 * 1.25 * T / E)
    cap += cap % 2
    assert B % 8 == 0

    with ExitStack() as es:
        def sb(name, shape, dt=F32):
            return es.enter_context(nc.sbuf_tensor(name, shape, dt))

        def sem(name):
            return es.enter_context(nc.semaphore(name))

        mask16 = nc.dram_tensor("mask16", [B, NK], F16, kind="Internal").ap()
        ps = es.enter_context(nc.psum_tensor("ps", [128, 8, BANK], F32))

        ident = sb("ident", [128, 128])
        negid = sb("negid", [PR, PR])
        hmask = sb("hmask", [SHIFT, 4], F16)
        sel = [sb(f"sel{l}", [128, NP]) for l in range(2)]
        selte = sb("selte", [128, NT])
        tri = sb("tri", [128, 128])
        real = sb("real", [128, 128])
        eidx = sb("eidx", [128, E])
        ones16 = sb("ones16", [128, CK], F16)
        xsq_full = sb("xsq", [128, max(NT, H), D])
        xsq = xsq_full[:, 0:NT, :]
        b2x_full = sb("b2x", [128, max(NT, H), D])
        b2x = b2x_full[:, 0:NT, :]
        wqT_s = xsq_full[0:DK0, 0:H, :]
        wkT_s = b2x_full[0:DK0, 0:H, :]
        g_s = sb("g_s", [D, H, D])
        wv_s = [sb(f"wv{l}", [D, D]) for l in range(2)]
        wvh = [sb(f"wvh{l}", [D, D], F16) for l in range(2)]
        wvl = [sb(f"wvl{l}", [D, D], F16) for l in range(2)]
        wk1_s = sb("wk1_s", [D, D])
        wk1h = sb("wk1h", [D, D], F16)
        wk1l = sb("wk1l", [D, D], F16)
        wq1_s = sb("wq1_s", [D, D])
        wq1r = sb("wq1r", [D, NG, 3, GW])
        bqr_s = sb("bqr_s", [SHIFT, NG])
        bqs = sb("bqs", [SHIFT, NG])
        bk_s = sb("bk_s", [D, 1])
        bv_s = sb("bv_s", [S + PB, D])
        wr_s = [sb(f"wr{l}", [D, E]) for l in range(2)]
        b1_s = sb("b1_s", [128, E, NF])
        b1e = sb("b1e", [128, NF])
        b2_s = sb("b2_s", [128, D])
        up_s = sb("up_s", [D, 2, FF])
        down_s = sb("down_s", [128, 2, NF, D])
        xs = sb("xs", [128, NT, D])
        xc = sb("xc", [128, NT, D])
        xT = sb("xT", [D, TOK])
        stat = sb("stat", [128, 8, NT])
        cn = sb("cn", [CK, 2, CH, D])
        cTh = sb("cTh", [D, 2, NK], F16)
        cTl = sb("cTl", [D, 2, NK], F16)
        vx = sb("vx", [CK, 2, CH, NP, 32])
        qh = sb("qh", [D, 2, COLS], F16)
        ql = sb("ql", [D, 2, COLS], F16)
        sh = sb("sh", [128, 2, COLS], F16)
        kh = sb("kh", [D, NK], F16)
        kl = sb("kl", [D, NK], F16)
        kst = sb("kst", [128, 2, NG, NK], F16)
        qst = sb("qst", [128, 2, COLS], F16)
        qc = sb("qc", [128, COLS], F16)
        qt = sb("qt", [SHIFT, NG, S])
        qhl = sb("qhl", [SHIFT, NG, S], F16)
        mf = sb("mf", [B, NK], F16)
        mp = sb("mp", [PR, NP, NKB])
        mx = sb("mx", [PR, 32])
        ring = sb("ring", [128, PROB * COLS])
        pt = ring[0:CK, :].rearrange("p (r n) -> p r n", r=PROB)
        rt = ring[:, 0:16 * NT * E].rearrange("p (k i e) -> p k i e", k=16, e=E)
        mi = ring[0:B, 0:NK].bitcast(I32)
        o_s = sb("o_s", [128, 2, PR])
        rden = sb("rden", [128, 2, 2, NG])
        on = sb("on", [128, D])
        hT = sb("hT", [128, 2, NF, 8, PB])
        gate = sb("gate", [128, NT, E])
        gateT = sb("gateT", [128, 128])
        zb = sb("zb", [128, 1])
        r1 = sb("r1", [128, 8, NT])

        loaded = [sem(f"loaded{i}") for i in range(2)]
        ready0 = sem("ready0")
        setup = sem("setup")
        g_ready = sem("g_ready")
        g_kept = sem("g_kept")
        ln_step = sem("ln_step")
        ln_var = sem("ln_var")
        ln_std = sem("ln_std")
        ln_xn = sem("ln_xn")
        xT_psum = sem("xT_psum")
        xT_kept = sem("xT_kept")
        stored = sem("stored")
        mf_kept = sem("mf_kept")
        mask_stored = sem("mask_stored")

        lay = []
        for l in range(2):
            u = UNITS0 if l == 0 else UNITS1
            n_units = sum(map(len, u))
            assert n_units % 3 == 0
            names = [name for c in u for name in c]
            n_high = sum(name[0] in ACT_READS[l] for name in names)
            n_free = sum(name[0] not in ACT_RELEASES[l] for name in names)
            lay.append(dict(
                units=u, n=n_units,
                ctx=[sem(f"ctx_loaded{l}{p}") for p in range(2)],
                filled=Signal(sem(f"unit_filled{l}"), n_units, -1),
                free=Signal(sem(f"unit_free{l}"), n_free, -1), names=names,
                high=Signal(sem(f"high_kept{l}"), n_high, -1),
                prep=Signal(sem(f"prep_step{l}"), 1 if l == 0 else 3, -1),
                scores=Signal(sem(f"scores_ready{l}"), CH, 0),
                probs=Signal(sem(f"probs_ready{l}"), CH, 0),
                pv=Signal(sem(f"pv_done{l}"), CH, 0),
                stack=[Signal(sem(f"keys_stacked{l}{g}"), 16 * 3, -1) for g in range(NG)],
                masked=Signal(sem(f"mask_row_loaded{l}"), 16, -1),
                spread=Signal(sem(f"queries_spread{l}"), 2, -1),
                o_kept=Signal(sem(f"o_kept{l}"), 1, 0),
                outT=Signal(sem(f"outT_ready{l}"), 1, 0),
                out=Signal(sem(f"out_step{l}"), 4 + l, 0),
            ))
        moe = []
        for l in range(2):
            moe.append(dict(
                wl=[sem(f"expert_loaded{l}{p}") for p in range(2)], up=sem(f"up_ready{l}"), act=sem(f"gelu_ready{l}"),
                dn=sem(f"down_ready{l}"), add=sem(f"down_added{l}"), lg=sem(f"logits_ready{l}"),
                rs=sem(f"route_step{l}"), lm=sem(f"logits_shifted{l}"), ex=sem(f"route_exp{l}"),
                ch=sem(f"choices_made{l}"), rp=sem(f"route_psum{l}"), bk=sem(f"bias_kept{l}"), gt=sem(f"gates_turned{l}"), rd=sem(f"routing_read{l}")))

        def unit_list(l):
            i = 0
            for c, names in enumerate(lay[l]["units"]):
                for name in names:
                    yield c, name, i
                    i += 1

        def index(l, name):
            return next(i for _, n, i in unit_list(l) if n == name)

        def wait_read(eng, l, st, i, back=0):
            L = lay[l]
            if i < 0:
                i, back = i + L["n"], back + 1
            by_act = L["names"][i][0] in ACT_RELEASES[l]
            which = ACT_READS[l] if by_act else None
            k = sum((name[0] in which) if by_act else (name[0] not in ACT_RELEASES[l]) for name in L["names"][:i + 1])
            L["high" if by_act else "free"].wait(eng, st, k, back)

        def steps(eng, body):
            body(Step(None, -1), 1, False, True)
            body(Step(None, 0), 0, True, True)
            body(Step(None, 1), 1, True, True)
            if NT > 2:
                with eng.Fori(1, NT - 1) as j:
                    body(Step(j, 0), 0, True, True)
                    body(Step(j, 1), 1, True, True)
            body(Step(None, B - 2), 0, True, True)
            body(Step(None, B - 1), 1, True, False)

        def tile_index(st, ahead):
            c = st.c + ahead
            return c // 2 if st.j is None else st.j + c // 2

        def vunit(l, k):
            n = 4 if l == 0 else 3
            return range(n * k, n * k + n)

        block = es.enter_context(nc.Block())

        N_LOADED = 16 * 25
        N_SETUP = 12

        @block.sync
        def _(sp):
            sp.wait_ge(ready0, 1)
            n0 = [0]

            def first(dst, src):
                n0[0] += 1
                sp.dma_start(dst, src).then_inc(loaded[0], 16)

            for p in range(2):
                first(xs[PB * p:PB * p + S, :, :], x.rearrange("(i p) s d -> p s i d", p=2)[p])
            first(ident[:], ident_d)
            first(wqT_s[:], wqT.rearrange("(h k) d -> k h d", k=DK0))
            first(wkT_s[:], wkT.rearrange("(h k) d -> k h d", k=DK0))
            first(wv_s[0][:], wv)
            for dst, src in ((negid, negid_d), (hmask, hmask_d), (sel[0], sel0_d), (sel[1], sel1_d),
                             (selte, selte_d), (tri, tri_d), (real, real_d), (eidx, eidx_d), (wr_s[0], wr0),
                             (b1_s, b1), (b2_s, b2rep), (wk1_s, wk1T), (wq1_s, wq1T), (bqr_s, bqr),
                             (bk_s, bk), (bv_s, bv), (wv_s[1], wv1T), (wr_s[1], wg), (mi, mask)):
                first(dst[:], src)

            def attention(l):
                L = lay[l]

                def load(st, ahead, par):
                    b = st.c + ahead if st.j is None else st.j * 2 + (st.c + ahead)
                    src = ctx_d[b] if st.j is None else ctx_d[bass.ds(b, 1)].squeeze(0)
                    sp.dma_start(cn[:, par], src.rearrange("(c p) d -> p c d", p=CK)).then_inc(L["ctx"][par], 16)

                def body(st, par):
                    if st.j is not None or st.c + 3 < B:
                        L["filled"].wait(sp, st, index(l, "T2") + 1)
                        load(st, 3, 1 - par)
                    if l == 1:
                        L["scores"].wait(sp, st, 0)
                        k = 1 - par
                        b = st.c + 1 if st.j is None else st.j * 2 + (st.c + 1)
                        row = mask16[b:b + 1, :] if st.j is None else mask16[bass.ds(b, 1), :]
                        sp.dma_start(kst[SHIFT:SHIFT + 1, k, :, :],
                                     row.unsqueeze(1).broadcast_to([1, NG, NK])).then_inc(L["masked"].sem, 16)
                        wait_read(sp, l, st, index(l, "K2"))
                        for g in range(NG):
                            for r, src in ((0, kh), (1, kl), (2, kh)):
                                sp.dma_start(kst[GW * r:GW * r + GW, k, g, :],
                                             src[GW * g:GW * g + GW, :]).then_inc(L["stack"][g].sem, 16)

                load(Step(None, 0), 0, 0)
                load(Step(None, 0), 1, 1)
                for s in (-1, 0, 1):
                    body(Step(None, s), s % 2)
                if NT > 3:
                    with sp.Fori(1, NT - 2) as j:
                        body(Step(j, 0), 0)
                        body(Step(j, 1), 1)
                for s in (B - 4, B - 3, B - 2):
                    body(Step(None, s), s % 2)

            def experts(l, up_d, down_d):
                M = moe[l]

                def load(e, p):
                    if isinstance(e, int):
                        a, b = up_d[e], down_d[e]
                    else:
                        a, b = up_d[bass.ds(e, 1)].squeeze(0), down_d[bass.ds(e, 1)].squeeze(0)
                    sp.dma_start(up_s[:, p], a).then_inc(M["wl"][p], 16)
                    sp.dma_start(down_s[:, p], b).then_inc(M["wl"][p], 16)

                load(0, 0)
                load(1, 1)
                with sp.Fori(1, E // 2) as j:
                    for p in range(2):
                        sp.wait_ge(M["dn"], (j * 2 + (p - 1)) * G)
                        load(j * 2 + p, p)

            attention(0)
            sp.wait_ge(mf_kept, 1)
            sp.dma_start(mask16, mf[:]).then_inc(mask_stored, 16)
            sp.wait_ge(mask_stored, 16)
            experts(0, w1, w2)
            attention(1)
            experts(1, fc, proj)
            sp.wait_ge(moe[1]["add"], E * G)
            for p in range(2):
                sp.dma_start(out.rearrange("(i p) s d -> p s i d", p=2)[p], xs[PB * p:PB * p + S, :, :]).then_inc(stored, 16)
            sp.wait_ge(stored, 32)

        @block.gpsimd
        def _(pool):
            pool.memset(xs[:], 0.0).then_inc(ready0, 1)
            pool.wait_ge(ready0, 1)
            fills = [(qc[SHIFT:128], 0.0), (qc[SHIFT:SHIFT + 1], TOPM / 2), (vx[:], 0.0), (vx[:, 0, :, :, 2 * W:2 * W + 1], 1.0), (vx[:, 1, :, :, 2 * W:2 * W + 1], 1.0),
                     (ones16[:], 1.0), (sh[:], 0.0), (kst[SHIFT:128], 1.0), (qst[SHIFT:128], 0.0), (mx[:], -TOPM),
                     (zb[:], 0.0), (hT[:], 0.0)]
            for n, (tile, value) in enumerate(fills):
                if n:
                    pool.wait_ge(setup, n)
                pool.memset(tile, value).then_inc(setup, 1)

            L = lay[1]

            def body(st, par, main, prep):
                if not prep:
                    return
                nb = 1 - par
                L["scores"].wait(pool, st, 0)
                pool.tensor_tensor(qst[SHIFT:128, nb, :], qc[SHIFT:128, :], qc[SHIFT:128, :], ALU.add).then_inc(L["spread"].sem, 1)
                L["prep"].wait(pool, st, 2)
                pool.tensor_tensor(qst[0:SHIFT, nb, :].rearrange("p (g i s) -> p g i s", g=NG, i=4),
                                   qhl[:].unsqueeze(2).broadcast_to([SHIFT, NG, 4, S]),
                                   hmask[:].unsqueeze(1).unsqueeze(3).broadcast_to([SHIFT, NG, 4, S]),
                                   ALU.mult).then_inc(L["spread"].sem, 1)

            pool.wait_ge(loaded[0], N_LOADED)
            pool.wait_ge(setup, N_SETUP)
            steps(pool, body)

        @block.scalar
        def _(act):
            act.wait_ge(setup, N_SETUP)

            def norm(n):
                act.wait_ge(ln_var, n + 1)
                act.activation(stat[:, 3, :], stat[:, 2, :], ACT.Sqrt).then_inc(ln_std, 1)

            def attention(l):
                L = lay[l]

                def body(st, par, main, prep):
                    nb = 1 - par
                    cur = 0
                    highs = 0
                    for c in range(CH):
                        if main:
                            L["scores"].wait(act, st, c + 1)
                            L["pv"].wait(act, st, c + 1 - PROB)
                            s2 = 2 * (c % 2)
                            act.activation(pt[:, c % PROB, :].rearrange("p (a n) -> p a n", a=2),
                                           ps[0:CK, s2:s2 + 2, 0:HB], ACT.Exp).then_inc(L["probs"].sem, 1)
                        if not prep:
                            continue
                        for name in L["units"][c]:
                            bank = 4 + cur % 3
                            cur += 1
                            k = int(name[1:] or 0)
                            if name[0] not in ACT_READS[l]:
                                continue
                            L["filled"].wait(act, st, cur)
                            highs += 1
                            if name[0] == "T":
                                act.activation(cTh[:, nb, KB * k:KB * k + KB], ps[:, bank, 0:KB],
                                               ACT.Copy).then_inc(L["high"].sem, 1)
                            elif name[0] == "Q":
                                act.activation(qh[:, nb, HB * k:HB * k + HB], ps[:, bank, 0:HB],
                                               ACT.Copy).then_inc(L["high"].sem, 1)
                            elif name[0] == "V":
                                if k == 0:
                                    L["pv"].wait(act, st, 0)
                                cs = vunit(l, k)
                                n = len(cs)
                                act.activation(vx[:, nb, cs[0]:cs[-1] + 1, :, 0:2 * W],
                                               ps[0:CK, bank, 0:128 * n].rearrange("p (c q w) -> p c q w", c=n, q=NP),
                                               ACT.Copy).then_inc(L["high"].sem, 1)
                            else:
                                if k == 0:
                                    for g in range(NG):
                                        L["stack"][g].wait(act, st, 0)
                                act.activation(kh[:, KB * k:KB * k + KB], ps[:, bank, 0:KB], ACT.Identity,
                                               bias=bk_s[:, 0:1]).then_inc(L["high"].sem, 1)

                steps(act, body)

            def experts(l):
                M = moe[l]
                act.wait_ge(M["lm"], 1)
                act.activation(rt[:, 2], rt[:, 1], ACT.Exp).then_inc(M["ex"], 1)

                def expert(e):
                    if l == 0:
                        if not isinstance(e, int):
                            act.wait_ge(M["act"], e * (G * NF))
                        be = b1_s[:, e, :] if isinstance(e, int) else b1_s[:, bass.ds(e, 1), :].squeeze(1)
                        act.activation(b1e[:], be, ACT.Copy).then_inc(M["bk"], 1)
                        act.wait_ge(M["bk"], e + 1)
                    for g in range(G):
                        for f in range(NF):
                            n = g * NF + f
                            act.wait_ge(M["up"], e * (G * NF) + (n + 1))
                            if f == 0 and (g > 1 or not isinstance(e, int)):
                                act.wait_ge(M["dn"], e * G + (g - 1))
                            o = hT[:, g % 2, f, :, 0:S]
                            i = ps[:, n % 4, 0:8 * S].rearrange("p (b s) -> p b s", s=S)
                            bias = b1e[:, f:f + 1] if l == 0 else zb[:, 0:1]
                            act.activation(o, i, ACT.Gelu, bias=bias).then_inc(M["act"], 1)

                expert(0)
                with act.Fori(1, E) as e:
                    expert(e)

            act.wait_ge(loaded[0], N_LOADED)
            norm(0)
            attention(0)
            norm(1)
            experts(0)
            norm(2)
            attention(1)
            norm(3)
            experts(1)

        @block.tensor
        def _(pe):
            pe.wait_ge(loaded[0], N_LOADED)
            pe.wait_ge(setup, N_SETUP)
            for h in range(H):
                mm = pe.matmul(ps[:, h // 4, 128 * (h % 4):128 * (h % 4) + 128], wqT_s[:, h, :], wkT_s[:, h, :],
                               start=True, stop=True)
                if h % 4 == 3:
                    mm.then_inc(g_ready, 1)

            def transpose_tokens(n):
                pe.wait_ge(ln_xn, n + 1)
                if n == 0:
                    pe.wait_ge(g_kept, 4)
                for i in range(NT):
                    mm = pe.transpose(ps[:, i // 4, 128 * (i % 4):128 * (i % 4) + 128], xc[:, i, :], ident[:])
                    if i % 4 == 3 or i == NT - 1:
                        mm.then_inc(xT_psum, 1)
                pe.wait_ge(xT_kept, (n + 1) * NX)

            NX = (NT + 3) // 4

            def attention(l):
                L = lay[l]

                def scores(st, par, c):
                    L["probs"].wait(pe, st, c - 1)
                    if l == 1 and c == 0:
                        wait_read(pe, l, st, -1)
                    for a in range(2):
                        cols = slice(HB * a, HB * a + HB)
                        o = ps[0:CK, 2 * (c % 2) + a, 0:HB]
                        ks = slice(CK * c, CK * c + CK)
                        if l == 0:
                            pe.matmul(o, cTh[:, par, ks], qh[:, par, cols], start=True, stop=False)
                            pe.matmul(o, cTh[:, par, ks], ql[:, par, cols], start=False, stop=False)
                            pe.matmul(o, cTl[:, par, ks], qh[:, par, cols], start=False, stop=False)
                        else:
                            for g in range(2 * a, 2 * a + 2):
                                mm = pe.matmul(ps[0:CK, 2 * (c % 2) + a, 224 * (g % 2):224 * (g % 2) + 224],
                                               kst[:, par, g, ks], qst[:, par, 224 * g:224 * g + 224],
                                               start=True, stop=True)
                    if l == 0:
                        if c == 0:
                            wait_read(pe, l, st, -1)
                        for a in range(2):
                            mm = pe.matmul(ps[0:CK, 2 * (c % 2) + a, 0:HB], ones16[:, :], sh[:, par, HB * a:HB * a + HB],
                                           start=False, stop=True)
                    mm.then_inc(L["scores"].sem, 1)

                def values(st, par, c, back):
                    L["probs"].wait(pe, st, c + 1, back=back)
                    if c == 0:
                        L["out"].wait(pe, st, L["out"].per, back=back + 1)
                    for p in range(NP):
                        j = p % 4
                        mm = pe.matmul(ps[32 * j:32 * j + 32, 7, PR * (p // 4):PR * (p // 4) + PR],
                                       vx[:, par, c, p, :], pt[:, c % PROB, PR * p:PR * p + PR],
                                       start=(c == 0 and p < 4), stop=(c == CH - 1), skip_group_check=True)
                    mm.then_inc(L["pv"].sem, 1)

                def turn_out(st, back):
                    L["o_kept"].wait(pe, st, 1, back=back)
                    base = PB * ((st.c - back) % 2)
                    for s in range(2):
                        for a in range(2):
                            n = 2 * s + a
                            mm = pe.matmul(ps[base:base + S, 7, 128 * n:128 * n + 128], o_s[:, s, S * a:S * a + S],
                                           ident[:, :], start=True, stop=True)
                    mm.then_inc(L["outT"].sem, 1)

                def unit(st, nb, name, i):
                    wait_read(pe, l, st, i - 3)
                    bank = 4 + i % 3
                    k = int(name[1:] or 0)
                    if name[0] == "T":
                        if k == 0:
                            pe.wait_ge(L["ctx"][nb], (tile_index(st, 1) + 1) * 16)
                        for q in range(4):
                            mm = pe.transpose(ps[:, bank, CK * q:CK * q + CK], cn[:, nb, 4 * k + q, :], ident[0:CK, 0:CK])
                    elif name[0] == "V":
                        if k == 0:
                            wait_read(pe, l, st, index(l, "T2"))
                        chunks = vunit(l, k)
                        for q, c in enumerate(chunks):
                            o = ps[0:CK, bank, 128 * q:128 * q + 128]
                            ks = slice(CK * c, CK * c + CK)
                            pe.matmul(o, cTh[:, nb, ks], wvh[l][:], start=True, stop=False)
                            pe.matmul(o, cTh[:, nb, ks], wvl[l][:], start=False, stop=False)
                            mm = pe.matmul(o, cTl[:, nb, ks], wvh[l][:], start=False, stop=True)
                    elif name[0] == "K":
                        wait_read(pe, l, st, index(l, f"T{k}"))
                        o = ps[:, bank, 0:KB]
                        ks = slice(KB * k, KB * k + KB)
                        pe.matmul(o, wk1h[:], cTh[:, nb, ks], start=True, stop=False)
                        pe.matmul(o, wk1h[:], cTl[:, nb, ks], start=False, stop=False)
                        mm = pe.matmul(o, wk1l[:], cTh[:, nb, ks], start=False, stop=True)
                    elif name[0] == "Q":
                        ti = tile_index(st, 1)
                        off = PB * nb
                        if isinstance(ti, int):
                            rhs = xT[:, 128 * ti + off:128 * ti + off + S]
                        else:
                            rhs = xT[:, bass.ds(ti * 128 + off, S)]
                        if l == 0:
                            for q in range(8):
                                mm = pe.matmul(ps[:, bank, S * q:S * q + S], g_s[:, 8 * k + q, :], rhs, start=True, stop=True)
                        else:
                            for g in range(NG):
                                mm = pe.matmul(ps[0:SHIFT, bank, S * g:S * g + S],
                                               wq1r[:, g].rearrange("p r w -> p (r w)"), rhs, start=True, stop=True)
                    elif name[0] == "M":
                        p, kb = divmod(k, NKB)
                        ks = slice(KB * kb, KB * kb + KB)
                        rows = slice(PR * p, PR * p + PR)
                        if l == 0:
                            if k == 0:
                                wait_read(pe, l, st, index(l, "Q1"))
                            mm = pe.matmul(ps[0:PR, bank, 0:KB], qh[:, nb, rows], cTh[:, nb, ks], start=True, stop=True)
                        else:
                            if k == 0:
                                L["spread"].wait(pe, st, 2)
                                L["masked"].wait(pe, st, 16)
                            if k % (2 * NKB) == 0:
                                L["stack"][p // 2].wait(pe, st, 16 * 3)
                            mm = pe.matmul(ps[0:PR, bank, 0:KB], qst[:, nb, rows], kst[:, nb, p // 2, ks],
                                           start=True, stop=True)
                    else:
                        L["prep"].wait(pe, st, L["prep"].per)
                        mm = pe.matmul(ps[SHIFT:SHIFT + NSH, bank, 0:PR], mx[:, 0:NSH], negid[:], start=True, stop=True)
                    mm.then_inc(L["filled"].sem, 1)

                def body(st, par, main, prep):
                    i = 0
                    for c in range(CH):
                        if main:
                            scores(st, par, c)
                            for v in PV_AT[c]:
                                if v >= 0:
                                    values(st, par, v, 0)
                                elif st.j is not None or st.c > 0:
                                    values(st, 1 - par, CH + v, 1)
                            if c == OUT_AT and (st.j is not None or st.c > 0):
                                turn_out(st, 1)
                        if prep:
                            for name in L["units"][c]:
                                unit(st, 1 - par, name, i)
                                i += 1
                    if main and not prep:
                        for c in (CH - 2, CH - 1):
                            values(st, par, c, 0)
                        turn_out(st, 0)

                steps(pe, body)

            def experts(l):
                M = moe[l]
                for i in range(NT):
                    mm = pe.matmul(ps[:, 7, E * i:E * i + E], xT[:, 128 * i:128 * i + 128], wr_s[l][:], start=True, stop=True)
                mm.then_inc(M["lg"], 1)
                pe.wait_ge(M["ch"], 1)
                if l == 0:
                    pe.transpose(ps[0:NT * E, 7, 0:128], gate[:].rearrange("p i e -> p (i e)"), ident[:]).then_inc(M["rp"], 1)
                    pe.wait_ge(M["gt"], 1)
                    for i in range(NT):
                        mm = pe.matmul(ps[:, i // 4, 128 * (i % 4):128 * (i % 4) + 128], gateT[0:NT * E, :], b2x[0:NT * E, i, :],
                                       start=True, stop=True)
                    mm.then_inc(M["rp"], 1)
                else:
                    for k in range(2):
                        oh = rt[:, 4 + k].rearrange("p i e -> p (i e)")
                        pe.matmul(ps[:, 7, 256 * k:256 * k + NT * E], tri[:], oh, start=True, stop=True)
                        mm = pe.matmul(ps[:, 7, 256 * k + 128:256 * k + 128 + NT * E], real[:], oh, start=True, stop=True)
                    mm.then_inc(M["rp"], 1)
                pe.wait_ge(M["rd"], 1)

                def up(e, par, g):
                    for f in range(NF):
                        n = g * NF + f
                        if n > 3 or not (isinstance(e, int) and e == 0):
                            pe.wait_ge(M["act"], e * (G * NF) + (n - 3))
                        rhs = xT[:, 512 * g:512 * g + 512].rearrange("p (b s) -> p b s", s=PB)[:, :, 0:S]
                        pe.matmul(ps[:, n % 4, 0:8 * S].rearrange("p (b s) -> p b s", s=S), up_s[:, par, 128 * f:128 * f + 128],
                                  rhs, start=True, stop=True).then_inc(M["up"], 1)

                def down(e, par, q):
                    pe.wait_ge(M["act"], e * (G * NF) + NF * (q + 1))
                    if q > 1 or not (isinstance(e, int) and e == 0):
                        pe.wait_ge(M["add"], e * G + (q - 1))
                    for t in range(4):
                        for f in range(NF):
                            lhs = hT[:, q % 2, f, 2 * t:2 * t + 2, :].rearrange("p b s -> p (b s)")
                            mm = pe.matmul(ps[:, 4 + q % 2, 128 * t:128 * t + 128], lhs, down_s[:, par, f, :],
                                           start=(f == 0), stop=(f == NF - 1))
                    mm.then_inc(M["dn"], 1)

                def expert(e, par):
                    first = isinstance(e, int) and e == 0
                    pe.wait_ge(M["wl"][par], 32 if isinstance(e, int) else e * 16 + (32 - 16 * par))
                    for g in range(G):
                        up(e, par, g)
                        if g > 0:
                            down(e, par, g - 1)
                        elif not first:
                            down(e - 1, 1 - par, G - 1)

                expert(0, 0)
                expert(1, 1)
                with pe.Fori(1, E // 2) as j:
                    expert(j * 2, 0)
                    expert(j * 2 + 1, 1)
                down(E - 1, 1, G - 1)

            transpose_tokens(0)
            attention(0)
            transpose_tokens(1)
            experts(0)
            transpose_tokens(2)
            attention(1)
            transpose_tokens(3)
            experts(1)

        @block.vector
        def _(dve):
            NX = (NT + 3) // 4
            dve.wait_ge(loaded[0], N_LOADED)
            dve.wait_ge(setup, N_SETUP)
            lns = [0]

            def link(ins):
                lns[0] += 1
                ins.then_inc(ln_step, 1)
                dve.wait_ge(ln_step, lns[0])

            for w, hi, lo in ((wv_s[0], wvh[0], wvl[0]), (wv_s[1], wvh[1], wvl[1]), (wk1_s, wk1h, wk1l)):
                link(dve.tensor_copy(hi[:], w[:]))
                link(dve.tensor_tensor(lo[:], w[:], hi[:], ALU.subtract))
            rs = float(1.0 / np.sqrt(np.float32(W)))
            for r in range(3):
                link(dve.tensor_scalar(wq1r[:, :, r, :], wq1_s[:].rearrange("p (g w) -> p g w", g=NG), rs, None, ALU.mult))
            link(dve.tensor_scalar(bqs[:], bqr_s[:], rs, None, ALU.mult))
            dve.tensor_scalar(mf[:], mi[:], -1.0, None, ALU.add).then_inc(mf_kept, 1)
            for n in range(4):
                dve.wait_ge(g_ready, n + 1)
                dve.tensor_scalar(g_s[:, 4 * n:4 * n + 4, :], ps[:, n, :].rearrange("p (h d) -> p h d", h=4),
                                  float(DK0) ** -0.5, None, ALU.mult).then_inc(g_kept, 1)
            link(dve.tensor_tensor(b2x[:], b2_s[:].unsqueeze(1).broadcast_to([128, NT, D]),
                                   selte[:].unsqueeze(2).broadcast_to([128, NT, D]), ALU.mult))

            def norm(n):
                link(dve.tensor_reduce(stat[:, 0, :], xs[:], AX.X, ALU.add))
                link(dve.tensor_scalar(stat[:, 1, :], stat[:, 0, :], 1.0 / D, None, ALU.mult))
                link(dve.tensor_tensor(xc[:], xs[:], stat[:, 1, :].unsqueeze(2).broadcast_to([128, NT, D]), ALU.subtract))
                link(dve.tensor_tensor(xsq[:], xc[:], xc[:], ALU.mult))
                link(dve.tensor_reduce(stat[:, 0, :], xsq[:], AX.X, ALU.add))
                dve.tensor_scalar(stat[:, 2, :], stat[:, 0, :], 1.0 / D, EPS, ALU.mult, ALU.add).then_inc(ln_var, 1)
                dve.wait_ge(ln_std, n + 1)
                link(dve.reciprocal(stat[:, 4, :], stat[:, 3, :]))
                link(dve.tensor_tensor(stat[:, 5, :], stat[:, 4, :], stat[:, 4, :], ALU.mult))
                link(dve.tensor_tensor(stat[:, 5, :], stat[:, 5, :], stat[:, 2, :], ALU.mult))
                link(dve.tensor_scalar(stat[:, 5, :], stat[:, 5, :], -0.5, 1.5, ALU.mult, ALU.add))
                link(dve.tensor_tensor(stat[:, 4, :], stat[:, 4, :], stat[:, 5, :], ALU.mult))
                dve.tensor_tensor(xc[:], xc[:], stat[:, 4, :].unsqueeze(2).broadcast_to([128, NT, D]),
                                  ALU.mult).then_inc(ln_xn, 1)
                for i in range(NX):
                    dve.wait_ge(xT_psum, n * NX + i + 1)
                    w = min(4, NT - 4 * i) * 128
                    dve.tensor_copy(xT[:, 512 * i:512 * i + w], ps[:, i, 0:w]).then_inc(xT_kept, 1)

            def attention(l):
                L = lay[l]

                def keep_sums(st, back):
                    L["pv"].wait(dve, st, CH, back=back)
                    dve.tensor_copy(o_s[:].rearrange("p s n -> p (s n)"), ps[:, 7, 0:2 * PR]).then_inc(L["o_kept"].sem, 1)

                def add_out(st, back):
                    base = PB * ((st.c - back) % 2)
                    rows = slice(base, base + S)
                    O = L["out"]
                    L["outT"].wait(dve, st, 1, back=back)
                    src = ps[rows, 7, :].rearrange("p (s a j w) -> p s a j w", s=2, a=2, j=NG)
                    dve.reciprocal(rden[rows], src[:, :, :, :, 2 * W]).then_inc(O.sem, 1)
                    O.wait(dve, st, 1, back=back)
                    dst = on[rows, :].rearrange("p (s j a w) -> p s a j w", s=2, j=NG, a=2)
                    for a in range(2):
                        dve.tensor_tensor(dst[:, :, a], src[:, :, a, :, W * a:W * a + W],
                                          rden[rows, :, a, :].unsqueeze(3).broadcast_to([S, 2, NG, W]),
                                          ALU.mult).then_inc(O.sem, 1)
                    k = 3
                    O.wait(dve, st, k, back=back)
                    if l == 1:
                        dve.tensor_tensor(on[rows], on[rows], bv_s[rows], ALU.add).then_inc(O.sem, 1)
                        k += 1
                        O.wait(dve, st, k, back=back)
                    ti = tile_index(st, -back)
                    xv = xs[rows, ti, :] if isinstance(ti, int) else xs[rows, bass.ds(ti, 1), :].squeeze(1)
                    dve.tensor_tensor(xv, xv, on[rows, :], ALU.add).then_inc(O.sem, 1)

                def unit(st, nb, name, i, highs):
                    F, P = L["free"], L["prep"]
                    if name[0] in ACT_RELEASES[l]:
                        return
                    L["filled"].wait(dve, st, i + 1)
                    bank = 4 + i % 3
                    k = int(name[1:] or 0)
                    if name[0] == "T":
                        ks = slice(KB * k, KB * k + KB)
                        L["high"].wait(dve, st, highs)
                        dve.tensor_tensor(cTl[:, nb, ks], ps[:, bank, 0:KB], cTh[:, nb, ks], ALU.subtract).then_inc(F.sem, 1)
                    elif name[0] == "V":
                        cs = vunit(l, k)
                        n = len(cs)
                        dve.tensor_copy(vx[:, nb, cs[0]:cs[-1] + 1, :, 0:2 * W],
                                        ps[0:CK, bank, 0:128 * n].rearrange("p (c q w) -> p c q w", c=n, q=NP)).then_inc(F.sem, 1)
                    elif name[0] == "K":
                        ks = slice(KB * k, KB * k + KB)
                        L["high"].wait(dve, st, highs)
                        dve.scalar_tensor_tensor(out=kl[:, ks], in0=ps[:, bank, 0:KB], scalar=bk_s[:, 0:1], in1=kh[:, ks],
                                                 op0=ALU.add, op1=ALU.subtract).then_inc(F.sem, 1)
                    elif name[0] == "Q" and l == 0:
                        cs = slice(HB * k, HB * k + HB)
                        L["high"].wait(dve, st, highs)
                        dve.tensor_tensor(ql[:, nb, cs], ps[:, bank, 0:HB], qh[:, nb, cs], ALU.subtract).then_inc(F.sem, 1)
                    elif name[0] == "Q":
                        dve.tensor_tensor(qt[:], ps[0:SHIFT, bank, 0:NG * S].rearrange("p (g s) -> p g s", g=NG),
                                          bqs[:].unsqueeze(2).broadcast_to([SHIFT, NG, S]), ALU.add).then_inc(F.sem, 1)
                        wait_read(dve, l, st, i)
                        dve.tensor_copy(qhl[:], qt[:]).then_inc(P.sem, 1)
                        P.wait(dve, st, 1)
                        dve.tensor_tensor(qhl[2 * GW:], qt[2 * GW:], qhl[2 * GW:], ALU.subtract).then_inc(P.sem, 1)
                    elif name[0] == "M":
                        p, kb = divmod(k, NKB)
                        dve.tensor_reduce(mp[:, p, kb:kb + 1], ps[0:PR, bank, 0:KB], AX.X, ALU.max).then_inc(F.sem, 1)
                        if k == 3 * NP - 1:
                            wait_read(dve, l, st, i)
                            dve.tensor_reduce(mx[:, 1:NSH], mp[:], AX.X, ALU.max).then_inc(P.sem, 1)
                    else:
                        dst = sh if l == 0 else qst
                        dve.tensor_tensor(dst[SHIFT:SHIFT + NSH, nb, :].rearrange("p (q n) -> p q n", q=NP),
                                          ps[SHIFT:SHIFT + NSH, bank, 0:PR].unsqueeze(1).broadcast_to([NSH, NP, PR]),
                                          sel[l][SHIFT:SHIFT + NSH, :].unsqueeze(2).broadcast_to([NSH, NP, PR]),
                                          ALU.mult).then_inc(F.sem, 1)

                def body(st, par, main, prep):
                    i = highs = 0
                    for c in range(CH):
                        if main and (st.j is not None or st.c > 0):
                            if c == 2:
                                keep_sums(st, 1)
                            if c == OUT_AT + 1:
                                add_out(st, 1)
                        if prep:
                            for name in L["units"][c]:
                                highs += name[0] in ACT_READS[l]
                                unit(st, 1 - par, name, i, highs)
                                i += 1
                    if main and not prep:
                        keep_sums(st, 0)
                        add_out(st, 0)
                        L["out"].wait(dve, st, L["out"].per)

                steps(dve, body)

            def experts(l):
                M = moe[l]
                n = [0]

                def link(ins):
                    n[0] += 1
                    ins.then_inc(M["rs"], 1)
                    dve.wait_ge(M["rs"], n[0])

                def wide(a):
                    return a.unsqueeze(2).broadcast_to([128, NT, E])

                ev = eidx[:].unsqueeze(1).broadcast_to([128, NT, E])

                def first_of(dst, values, scratch, m):
                    link(dve.tensor_reduce(m, values, AX.X, ALU.max))
                    link(dve.tensor_tensor(scratch, values, wide(m), ALU.is_equal))
                    link(dve.tensor_tensor(scratch, scratch, ev, ALU.mult))
                    link(dve.tensor_reduce(m, scratch, AX.X, ALU.max))
                    link(dve.tensor_tensor(dst, scratch, wide(m), ALU.is_equal))

                lg = ps[:, 7, 0:NT * E].rearrange("p (i e) -> p i e", e=E)
                dve.wait_ge(M["lg"], 1)
                link(dve.tensor_copy(rt[:, 0], lg))
                link(dve.tensor_reduce(r1[:, 0], rt[:, 0], AX.X, ALU.max))
                dve.tensor_tensor(rt[:, 1], rt[:, 0], wide(r1[:, 0]), ALU.subtract).then_inc(M["lm"], 1)
                dve.wait_ge(M["ex"], 1)
                if l == 0:
                    first_of(rt[:, 4], rt[:, 2], rt[:, 3], r1[:, 1])
                    link(dve.tensor_reduce(r1[:, 2], rt[:, 2], AX.X, ALU.add))
                    link(dve.tensor_reduce(r1[:, 4], rt[:, 2], AX.X, ALU.max))
                    link(dve.reciprocal(r1[:, 3], r1[:, 2]))
                    link(dve.tensor_tensor(r1[:, 3], r1[:, 3], r1[:, 4], ALU.mult))
                    dve.tensor_tensor(gate[:], rt[:, 4], wide(r1[:, 3]), ALU.mult).then_inc(M["ch"], 1)
                    dve.wait_ge(M["rp"], 1)
                    dve.tensor_copy(gateT[0:NT * E, :], ps[0:NT * E, 7, 0:128]).then_inc(M["gt"], 1)
                    dve.wait_ge(M["rp"], 2)
                    for i in range(NX):
                        k = min(4, NT - 4 * i)
                        xv = xs[:, 4 * i:4 * i + k, :]
                        ins = dve.tensor_tensor(xv, xv, ps[:, i, 0:128 * k].rearrange("p (t d) -> p t d", d=D), ALU.add)
                        if i < NX - 1:
                            link(ins)
                    ins.then_inc(M["rd"], 1)
                else:
                    first_of(rt[:, 4], rt[:, 1], rt[:, 3], r1[:, 1])
                    link(dve.scalar_tensor_tensor(out=rt[:, 6], in0=rt[:, 4], scalar=-3.0e38, in1=rt[:, 1],
                                                  op0=ALU.mult, op1=ALU.add))
                    first_of(rt[:, 5], rt[:, 6], rt[:, 3], r1[:, 2])
                    link(dve.tensor_tensor(rt[:, 8], rt[:, 2], rt[:, 5], ALU.mult))
                    link(dve.tensor_reduce(r1[:, 4], rt[:, 8], AX.X, ALU.add))
                    link(dve.tensor_scalar(r1[:, 5], r1[:, 4], 1.0, None, ALU.add))
                    link(dve.reciprocal(r1[:, 6], r1[:, 5]))
                    dve.tensor_tensor(r1[:, 7], r1[:, 4], r1[:, 6], ALU.mult).then_inc(M["ch"], 1)
                    dve.wait_ge(M["rp"], 1)
                    for k in range(2):
                        pre = ps[:, 7, 256 * k:256 * k + NT * E].rearrange("p (i e) -> p i e", e=E)
                        tot = ps[:, 7, 256 * k + 128:256 * k + 128 + NT * E].rearrange("p (i e) -> p i e", e=E)
                        a, b = 8, 9
                        link(dve.tensor_copy(rt[:, a], tot))
                        d = 1
                        while d < NT:
                            link(dve.tensor_copy(rt[:, b, 0:d], rt[:, a, 0:d]))
                            link(dve.tensor_tensor(rt[:, b, d:NT], rt[:, a, d:NT], rt[:, a, 0:NT - d], ALU.add))
                            a, b, d = b, a, 2 * d
                        if k == 0:
                            link(dve.tensor_copy(rt[:, 12, 0:1], rt[:, a, NT - 1:NT]))
                        link(dve.tensor_tensor(rt[:, 10], rt[:, a], tot, ALU.subtract))
                        link(dve.tensor_tensor(rt[:, 10], rt[:, 10], pre, ALU.add))
                        if k == 1:
                            link(dve.tensor_tensor(rt[:, 10], rt[:, 10], rt[:, 12, 0:1, :].broadcast_to([128, NT, E]), ALU.add))
                        link(dve.scalar_tensor_tensor(out=rt[:, 11], in0=rt[:, 10], scalar=float(cap), in1=rt[:, 4 + k],
                                                      op0=ALU.is_lt, op1=ALU.mult))
                        link(dve.tensor_tensor(rt[:, 13 + k], rt[:, 11], wide(r1[:, 6 + k]), ALU.mult))
                    dve.tensor_tensor(gate[:], rt[:, 13], rt[:, 14], ALU.add).then_inc(M["rd"], 1)
                dve.wait_ge(M["rd"], 1)

                def expert(e):
                    for g in range(G):
                        dve.wait_ge(M["dn"], e * G + (g + 1))
                        if not isinstance(e, int):
                            dve.wait_ge(M["add"], (e - 1) * G + (g + 1))
                        bank = 4 + g % 2
                        for t in range(4):
                            i = 4 * g + t
                            ins = dve.scalar_tensor_tensor(out=xs[:, i, :], in0=ps[:, bank, 128 * t:128 * t + 128],
                                                           scalar=gate[:, i, e:e + 1] if isinstance(e, int) else gate[:, i, bass.ds(e, 1)], in1=xs[:, i, :],
                                                           op0=ALU.mult, op1=ALU.add)
                        ins.then_inc(M["add"], 1)

                expert(0)
                with dve.Fori(1, E) as e:
                    expert(e)
                dve.wait_ge(M["add"], E * G)

            norm(0)
            attention(0)
            norm(1)
            experts(0)
            norm(2)
            attention(1)
            norm(3)
            experts(1)



_IN = ["x", "ctx", "mask", "wqT", "wkT", "wv", "wr0", "w1", "b1", "w2", "b2rep", "wq1T", "bqr", "wk1T", "bk", "wv1T", "bv",
       "wg", "fc", "proj", "ident", "negid", "hmask", "sel0", "sel1", "selte", "tri", "real", "eidx"]


def constants(NT):
    p = np.arange(128)
    is_real = (p % PB) < S
    sel1 = np.zeros((128, NP), np.float32)
    for t in range(NP):
        sel1[SHIFT + 1 + t, t] = 1
    sel0 = sel1.copy()
    sel1[SHIFT] = 1
    return dict(
        ident=np.eye(128, dtype=np.float32), negid=-np.eye(PR, dtype=np.float32),
        hmask=((p[:SHIFT, None] % GW) // W == np.arange(4)).astype(np.float16), sel0=sel0, sel1=sel1,
        selte=(p[:, None] // E == np.arange(NT)).astype(np.float32),
        tri=((p[:, None] < p[None]) & is_real[:, None]).astype(np.float32),
        real=np.repeat(is_real[:, None], 128, 1).astype(np.float32),
        eidx=np.repeat((E - np.arange(E, dtype=np.float32))[None], 128, 0))


def laid_out(i):
    a = {k: np.asarray(v) for k, v in i.items()}
    B = a["x"].shape[0]
    NT = B // 2
    d = dict(
        x=a["x"], ctx=a["ctx_1024"], mask=a["mask_BxS2_ik0"], wqT=a["L0_xattn_wq"].T, wkT=a["L0_xattn_wk"].T,
        wv=a["L0_xattn_wv"], wr0=a["L0_ffn_Wr"], w1=a["L0_ffn_W1"],
        b1=a["L0_ffn_b1"].reshape(E, NF, 128).transpose(2, 0, 1),
        w2=a["L0_ffn_W2"].reshape(E, NF, 128, D).transpose(0, 2, 1, 3), b2rep=np.tile(a["L0_ffn_b2"], (128 // E, 1)),
        wq1T=a["L1_xattn_Wq"].T, bqr=np.tile(a["L1_xattn_bq"].reshape(NG, GW).T, (3, 1)), wk1T=a["L1_xattn_Wk"].T,
        bk=a["L1_xattn_bk"].reshape(D, 1), wv1T=a["L1_xattn_Wv"].T, bv=np.tile(a["L1_xattn_bv"][None], (S + PB, 1)),
        wg=a["L1_ffn_w_g"], fc=a["L1_ffn_c_fc"], proj=a["L1_ffn_c_proj"].reshape(E, NF, 128, D).transpose(0, 2, 1, 3))
    d.update(constants(NT))
    return B, {k: np.ascontiguousarray(v) for k, v in d.items()}


def kernel(**inputs):
    import concourse.bacc as bacc
    from concourse.bass_utils import run_bass_kernel_spmd

    B, arrays = laid_out(inputs)
    nc = bacc.Bacc("TRN2", target_bir_lowering=False, num_devices=1)
    arrays = {"in_" + n: a for n, a in arrays.items()}
    args = [nc.dram_tensor(n, arrays[n].shape, mybir.dt.from_np(arrays[n].dtype), kind="ExternalInput").ap() for n in ("in_" + n for n in _IN)]
    out = nc.dram_tensor("out", [B, S, D], F32, kind="ExternalOutput").ap()
    program(nc, B, args, out)
    r = run_bass_kernel_spmd(nc, [arrays], core_ids=[0])
    return r.results[0]["out"]
```

```python
from contextlib import ExitStack

import numpy as np

import concourse.bass as bass
from concourse import mybir

F32 = mybir.dt.float32
F16 = mybir.dt.float16
I32 = mybir.dt.int32
ALU = mybir.AluOpType
ACT = mybir.ActivationFunctionType
AX = mybir.AxisListType

S, D = 56, 128
NK, CH = 1500, 12
CK = NK // CH
H = 16
DK0 = 64
W = D // H
NP = H // 2
PR = 2 * S
NG = 4
GW = D // NG
COLS = H * S
HB = COLS // 2
BANK = 512
KB = 500
NKB = NK // KB
PB = 64
E, FF = 8, 512
NF = FF // 128
SHIFT = 96
NSH = 1 + NP
TOPM = 10000.0
PROB = 6
EPS = 1e-5

def numbered(text):
    m, out = 0, []
    for chunk in text.split("|"):
        out.append([])
        for name in chunk.split():
            if name == "M":
                name, m = f"M{m}", m + 1
            out[-1].append(name)
    assert m == NP * NKB and len(out) == CH
    return out


UNITS0 = numbered("T0 T1 | T2 Q0 | Q1 V0 | V1 M M M | V2 M M M | M M M | M M M | M M M | M M M | M M M | M M M | R")
UNITS1 = numbered("T0 M T1 | M V0 M V1 | M T2 M | K0 M M | V2 M M V3 | K1 M M | M Q0 M M | M K2 M | M M M | M M M | M M | R")
UNITS_FIRST = [False, True]
AHEAD1 = "TKQ"
FIRST1 = [[n for n in c if n[0] in AHEAD1] for c in UNITS1]
LAST1 = [[n for n in c if n[0] not in AHEAD1] for c in UNITS1]
ACT_READS = ["TQ", "TKV"]
ACT_RELEASES = ["", "TKV"]
PARTS1 = [(0, 2), (2, 3)]
PART_AT = [k0 for k0, k1 in PARTS1]


def max_unit(l, k):
    if l == 0:
        return divmod(k, NKB)
    n = PARTS1[0][1]
    return divmod(k, n) if k < n * NP else (k - n * NP, n)


PV_AT = [[[-2], [-1], [], [], [0], [1, 2], [3, 4], [5], [6], [7], [8], [9]],
         [[-2], [-1], [], [], [], [0, 1], [2], [3, 4], [5], [6, 7], [8], [9]]]
OUT_AT = 3


class Step:

    def __init__(self, j, c):
        self.j, self.c = j, c

    def value(self, per, k, back=0):
        c = (self.c - back) * per + k
        return c if self.j is None else self.j * (2 * per) + c


class Signal:

    def __init__(self, sem, per, first, lead=0):
        self.sem, self.per, self.first, self.lead = sem, per, first, lead

    def wait(self, eng, st, k, back=0):
        if st.j is None and st.c - back < self.first:
            v = k if st.c - back == self.first - 1 and self.lead else 0
        else:
            v = self.lead + st.value(self.per, k, back + self.first)
        if st.j is not None or v > 0:
            eng.wait_ge(self.sem, v)


def program(nc, B, args, out):
    (x, ctx_d, mask, wqT, wkT, wv, wr0, w1, b1, w2, b2rep, wq1T, bqr, wk1T, bk, wv1T, bv, wg, fc,
     proj, ident_d, negid_d, hmask_d, sel0_d, sel1_d, selte_d, tri_d, real_d, eidx_d) = args
    NT = B // 2
    TOK = NT * 128
    G = B // 8
    T = B * S
    cap = int(2 * 1.25 * T / E)
    cap += cap % 2
    assert B % 8 == 0

    with ExitStack() as es:
        def sb(name, shape, dt=F32):
            return es.enter_context(nc.sbuf_tensor(name, shape, dt))

        def sem(name):
            return es.enter_context(nc.semaphore(name))

        mask16 = nc.dram_tensor("mask16", [B, NK], F16, kind="Internal").ap()
        ps = es.enter_context(nc.psum_tensor("ps", [128, 8, BANK], F32))

        ident = sb("ident", [128, 128])
        negid = sb("negid", [PR, PR])
        hmask = sb("hmask", [SHIFT, 4], F16)
        sel = [sb(f"sel{l}", [128, NP]) for l in range(2)]
        selte = sb("selte", [128, NT])
        tri = sb("tri", [128, 128])
        real = sb("real", [128, 128])
        eidx = sb("eidx", [128, E])
        ones16 = sb("ones16", [128, CK], F16)
        xsq_full = sb("xsq", [128, max(NT, H), D])
        xsq = xsq_full[:, 0:NT, :]
        b2x_full = sb("b2x", [128, max(NT, H), D])
        b2x = b2x_full[:, 0:NT, :]
        wqT_s = xsq_full[0:DK0, 0:H, :]
        wkT_s = b2x_full[0:DK0, 0:H, :]
        g_s = sb("g_s", [D, H, D])
        wv_s = [sb(f"wv{l}", [D, D]) for l in range(2)]
        wvh = [sb(f"wvh{l}", [D, D], F16) for l in range(2)]
        wvl = [sb(f"wvl{l}", [D, D], F16) for l in range(2)]
        wk1_s = sb("wk1_s", [D, D])
        wk1h = sb("wk1h", [D, D], F16)
        wk1l = sb("wk1l", [D, D], F16)
        wq1_s = sb("wq1_s", [D, D])
        wq1r = sb("wq1r", [D, NG, 3, GW])
        bqr_s = sb("bqr_s", [SHIFT, NG])
        bqs = sb("bqs", [SHIFT, NG])
        bk_s = sb("bk_s", [D, 1])
        bv_s = sb("bv_s", [S + PB, D])
        wr_s = [sb(f"wr{l}", [D, E]) for l in range(2)]
        b1_s = sb("b1_s", [128, E, NF])
        b1e = sb("b1e", [128, NF])
        b2_s = sb("b2_s", [128, D])
        up_s = sb("up_s", [D, 2, FF])
        down_s = sb("down_s", [128, 2, NF, D])
        xs = sb("xs", [128, NT, D])
        xc = sb("xc", [128, NT, D])
        xT = sb("xT", [D, TOK])
        stat = sb("stat", [128, 8, NT])
        cn = sb("cn", [CK, 2, CH, D])
        cTh = sb("cTh", [D, 2, NK], F16)
        cTl = sb("cTl", [D, 2, NK], F16)
        vx = sb("vx", [CK, 2, CH, NP, 32])
        qh = sb("qh", [D, 2, COLS], F16)
        ql = sb("ql", [D, 2, COLS], F16)
        sh = sb("sh", [128, 2, COLS], F16)
        kh = sb("kh", [D, NK], F16)
        kl = sb("kl", [D, NK], F16)
        kst = sb("kst", [128, 2, NG, NK], F16)
        qst = sb("qst", [128, 2, COLS], F16)
        full = sb("full", [128, 2, KB])
        qt = sb("qt", [SHIFT, NG, S])
        qhl = sb("qhl", [SHIFT, NG, S], F16)
        mf = sb("mf", [B, NK], F16)
        mp = sb("mp", [PR, NP, NKB])
        mx = sb("mx", [PR, 32])
        ring = sb("ring", [128, PROB * COLS])
        pt = ring[0:CK, :].rearrange("p (r n) -> p r n", r=PROB)
        rt = ring[:, 0:16 * NT * E].rearrange("p (k i e) -> p k i e", k=16, e=E)
        mi = ring[0:B, 0:NK].bitcast(I32)
        o_s = sb("o_s", [128, 2, PR])
        rden = sb("rden", [128, 2, 2, NG])
        on = sb("on", [128, D])
        hT = sb("hT", [128, 2, NF, 8, PB])
        gate = sb("gate", [128, NT, E])
        gateT = sb("gateT", [128, 128])
        zb = sb("zb", [128, 1])
        r1 = sb("r1", [128, 8, NT])

        loaded = [sem(f"loaded{i}") for i in range(2)]
        ready0 = sem("ready0")
        setup = sem("setup")
        g_ready = sem("g_ready")
        g_kept = sem("g_kept")
        ln_step = sem("ln_step")
        ln_var = sem("ln_var")
        ln_std = sem("ln_std")
        ln_xn = sem("ln_xn")
        xT_psum = sem("xT_psum")
        xT_kept = sem("xT_kept")
        stored = sem("stored")
        mf_kept = sem("mf_kept")
        mask_stored = sem("mask_stored")

        def act_signals(l, name):
            return (name[0] in ACT_READS[l]) 

        lay = []
        for l in range(2):
            u = UNITS0 if l == 0 else UNITS1
            n_units = sum(map(len, u))
            assert n_units % 3 == 0
            names = [name for c in u for name in c]
            n_high = sum(act_signals(l, name) for name in names)
            n_free = sum(name[0] not in ACT_RELEASES[l] for name in names)
            ahead = [name for c in FIRST1 for name in c] if l == 1 else []
            lay.append(dict(
                n=n_units,
                ctx=[sem(f"ctx_loaded{l}{p}") for p in range(2)],
                filled=Signal(sem(f"unit_filled{l}"), n_units, -1, len(ahead)),
                free=Signal(sem(f"unit_free{l}"), n_free, -1, sum(name[0] not in ACT_RELEASES[l] for name in ahead)),
                high=Signal(sem(f"high_kept{l}"), n_high, -1, sum(act_signals(l, name) for name in ahead)),
                low=Signal(sem(f"low_kept{l}"), 12, -1, 12),
                prep=Signal(sem(f"prep_step{l}"), 1 + 2 * l, -1, 2 * l),
                scores=Signal(sem(f"scores_ready{l}"), CH, 0),
                probs=Signal(sem(f"probs_ready{l}"), CH, 0),
                pv=Signal(sem(f"pv_done{l}"), CH, 0),
                stack=[[Signal(sem(f"keys_stacked{l}{h}{g}"), 16 * 3, -2) for g in range(NG)] for h in range(2)],
                masked=[Signal(sem(f"mask_row_loaded{l}{h}"), 16, -2) for h in range(2)],
                spread=Signal(sem(f"queries_spread{l}"), 1, -1),
                o_kept=Signal(sem(f"o_kept{l}"), 1, 0),
                outT=Signal(sem(f"outT_ready{l}"), 1, 0),
                out=Signal(sem(f"out_step{l}"), 4 + l, 0),
            ))
        moe = []
        for l in range(2):
            moe.append(dict(
                wl=[sem(f"expert_loaded{l}{p}") for p in range(2)], up=sem(f"up_ready{l}"), act=sem(f"gelu_ready{l}"),
                dn=sem(f"down_ready{l}"), add=sem(f"down_added{l}"), lg=sem(f"logits_ready{l}"),
                rs=sem(f"route_step{l}"), lm=sem(f"logits_shifted{l}"), ex=sem(f"route_exp{l}"),
                ch=sem(f"choices_made{l}"), rp=sem(f"route_psum{l}"), bk=sem(f"bias_kept{l}"), gt=sem(f"gates_turned{l}"), rd=sem(f"routing_read{l}")))

        def plan(l, st, back=0):
            if l == 0:
                return UNITS0
            if st.j is None and st.c - back == -2:
                return FIRST1
            if st.j is None and st.c - back == B - 2:
                return LAST1
            return UNITS1

        def names_of(l, st, back=0):
            return [name for c in plan(l, st, back) for name in c]

        def index(l, st, name, back=0):
            return names_of(l, st, back).index(name)

        def batch_of(l, par, name):
            return (2, par) if l == 1 and name[0] in AHEAD1 else (1, 1 - par)

        def prep_count(l, st, name, back=0):
            before = names_of(l, st, back)
            before = before[:before.index(name)]
            return 2 * l * ("Q0" in before) + (f"M{NP * NKB - 1}" in before)

        def bank_of(l, st, i):
            return 4 + (i - len(names_of(l, st)) % 3 if plan(l, st) is FIRST1 else i) % 3

        def wait_read(eng, l, st, i, back=0):
            L = lay[l]
            if isinstance(i, int) and i < 0:
                back += 1
                if st.j is None and st.c - back < (-1 if l == 0 else -2):
                    return
                i += len(names_of(l, st, back))
            names = names_of(l, st, back)
            if isinstance(i, str):
                i = names.index(i)
            by_act = names[i][0] in ACT_RELEASES[l]
            k = sum(act_signals(l, name) if by_act else (name[0] not in ACT_RELEASES[l]) for name in names[:i + 1])
            L["high" if by_act else "free"].wait(eng, st, k, back)

        def low_index(name):
            return "T0 T1 T2 K0 K1 K2".split().index(name)

        def steps(eng, body, l):
            if l == 1:
                body(Step(None, -2), 0, False, True)
            body(Step(None, -1), 1, False, True)
            body(Step(None, 0), 0, True, True)
            body(Step(None, 1), 1, True, True)
            if NT > 2:
                with eng.Fori(1, NT - 1) as j:
                    body(Step(j, 0), 0, True, True)
                    body(Step(j, 1), 1, True, True)
            body(Step(None, B - 2), 0, True, True)
            body(Step(None, B - 1), 1, True, False)

        def tile_index(st, ahead):
            c = st.c + ahead
            return c // 2 if st.j is None else st.j + c // 2

        def vunit(l, k):
            n = 4 if l == 0 else 3
            return range(n * k, n * k + n)

        block = es.enter_context(nc.Block())

        N_LOADED = 16 * 25
        N_SETUP = 11

        @block.sync
        def _(sp):
            sp.wait_ge(ready0, 1)
            n0 = [0]

            def first(dst, src):
                n0[0] += 1
                sp.dma_start(dst, src).then_inc(loaded[0], 16)

            for p in range(2):
                first(xs[PB * p:PB * p + S, :, :], x.rearrange("(i p) s d -> p s i d", p=2)[p])
            first(ident[:], ident_d)
            first(wqT_s[:], wqT.rearrange("(h k) d -> k h d", k=DK0))
            first(wkT_s[:], wkT.rearrange("(h k) d -> k h d", k=DK0))
            first(wv_s[0][:], wv)
            for dst, src in ((negid, negid_d), (hmask, hmask_d), (sel[0], sel0_d), (sel[1], sel1_d),
                             (selte, selte_d), (tri, tri_d), (real, real_d), (eidx, eidx_d), (wr_s[0], wr0),
                             (b1_s, b1), (b2_s, b2rep), (wk1_s, wk1T), (wq1_s, wq1T), (bqr_s, bqr),
                             (bk_s, bk), (bv_s, bv), (wv_s[1], wv1T), (wr_s[1], wg), (mi, mask)):
                first(dst[:], src)

            def attention(l):
                L = lay[l]

                def load(st, ahead, par):
                    b = st.c + ahead if st.j is None else st.j * 2 + (st.c + ahead)
                    src = ctx_d[b] if st.j is None else ctx_d[bass.ds(b, 1)].squeeze(0)
                    sp.dma_start(cn[:, par], src.rearrange("(c p) d -> p c d", p=CK)).then_inc(L["ctx"][par], 16)

                def body(st, par):
                    far = 3 + l
                    to = 1 - par if l == 0 else par
                    if st.j is not None or st.c + far < B:
                        L["filled"].wait(sp, st, index(l, st, "T2") + 1)
                        load(st, far, to)
                    if l == 1:
                        b = st.c + 2 if st.j is None else st.j * 2 + (st.c + 2)
                        for h, (k0, k1) in enumerate(PARTS1):
                            ks = slice(KB * k0, KB * k1)
                            row = mask16[b:b + 1, ks] if st.j is None else mask16[bass.ds(b, 1), ks]
                            L["scores"].wait(sp, st, KB * k1 // CK)
                            if st.j is None and st.c == -1:
                                L["filled"].wait(sp, st, index(l, st, f"M{NP * NKB - 1}") + 1)
                            sp.dma_start(kst[SHIFT:SHIFT + 1, par, :, ks],
                                         row.unsqueeze(1).broadcast_to([1, NG, KB * (k1 - k0)])).then_inc(L["masked"][h].sem, 16)
                            L["low"].wait(sp, st, 2 * low_index(f"K{k1 - 1}") + 2)
                            for g in range(NG):
                                for r, src in ((0, kh), (1, kl), (2, kh)):
                                    sp.dma_start(kst[GW * r:GW * r + GW, par, g, ks],
                                                 src[GW * g:GW * g + GW, ks]).then_inc(L["stack"][h][g].sem, 16)

                load(Step(None, 0), 0, 0)
                load(Step(None, 0), 1, 1)
                for s in range(-1 - l, 2):
                    body(Step(None, s), s % 2)
                if NT > 3:
                    with sp.Fori(1, NT - 2) as j:
                        body(Step(j, 0), 0)
                        body(Step(j, 1), 1)
                for s in range(B - 4, B - 3 + l):
                    body(Step(None, s), s % 2)

            def experts(l, up_d, down_d):
                M = moe[l]

                def load(e, p):
                    if isinstance(e, int):
                        a, b = up_d[e], down_d[e]
                    else:
                        a, b = up_d[bass.ds(e, 1)].squeeze(0), down_d[bass.ds(e, 1)].squeeze(0)
                    sp.dma_start(up_s[:, p], a).then_inc(M["wl"][p], 16)
                    sp.dma_start(down_s[:, p], b).then_inc(M["wl"][p], 16)

                load(0, 0)
                load(1, 1)
                with sp.Fori(1, E // 2) as j:
                    for p in range(2):
                        sp.wait_ge(M["dn"], (j * 2 + (p - 1)) * G)
                        load(j * 2 + p, p)

            attention(0)
            sp.wait_ge(mf_kept, 1)
            sp.dma_start(mask16, mf[:]).then_inc(mask_stored, 16)
            sp.wait_ge(mask_stored, 16)
            experts(0, w1, w2)
            attention(1)
            experts(1, fc, proj)
            sp.wait_ge(moe[1]["add"], E * G)
            for p in range(2):
                sp.dma_start(out.rearrange("(i p) s d -> p s i d", p=2)[p], xs[PB * p:PB * p + S, :, :]).then_inc(stored, 16)
            sp.wait_ge(stored, 32)

        @block.gpsimd
        def _(pool):
            pool.memset(xs[:], 0.0).then_inc(ready0, 1)
            pool.wait_ge(ready0, 1)
            fills = [(vx[:], 0.0), (vx[:, 0, :, :, 2 * W:2 * W + 1], 1.0), (vx[:, 1, :, :, 2 * W:2 * W + 1], 1.0),
                     (ones16[:], 1.0), (sh[:], 0.0), (kst[SHIFT:128], 1.0), (qst[SHIFT:128], 0.0), (qst[SHIFT:SHIFT + 1], TOPM), (mx[:], -TOPM),
                     (zb[:], 0.0), (hT[:], 0.0)]
            for n, (tile, value) in enumerate(fills):
                if n:
                    pool.wait_ge(setup, n)
                pool.memset(tile, value).then_inc(setup, 1)

            L = lay[1]

            def body(st, par, main, prep):
                if not prep:
                    return
                names = names_of(1, st)
                if "R" in names:
                    nb = 1 - par
                    L["scores"].wait(pool, st, 0)
                    L["prep"].wait(pool, st, prep_count(1, st, "Q0", 1) + 2, back=1)
                    pool.tensor_tensor(qst[0:SHIFT, nb, :].rearrange("p (g i s) -> p g i s", g=NG, i=4),
                                       qhl[:].unsqueeze(2).broadcast_to([SHIFT, NG, 4, S]),
                                       hmask[:].unsqueeze(1).unsqueeze(3).broadcast_to([SHIFT, NG, 4, S]),
                                       ALU.mult).then_inc(L["spread"].sem, 1)
                copies = 0
                for name in names:
                    copies += act_signals(1, name)
                    if name[0] in "TK":
                        k, n = int(name[1]), low_index(name)
                        ks = slice(KB * k, KB * k + KB)
                        hi, lo = (cTh[:, par, ks], cTl[:, par, ks]) if name[0] == "T" else (kh[:, ks], kl[:, ks])
                        if name[0] == "K" and k in PART_AT:
                            for g in range(NG):
                                L["stack"][PART_AT.index(k)][g].wait(pool, st, 0)
                        L["high"].wait(pool, st, copies)
                        pool.tensor_tensor(hi, full[:, n % 2, :], zb[:].broadcast_to([128, KB]), ALU.add).then_inc(L["low"].sem, 1)
                        L["low"].wait(pool, st, 2 * n + 1)
                        pool.tensor_tensor(lo, full[:, n % 2, :], hi, ALU.subtract).then_inc(L["low"].sem, 1)

            pool.wait_ge(loaded[0], N_LOADED)
            pool.wait_ge(setup, N_SETUP)
            steps(pool, body, 1)

        @block.scalar
        def _(act):
            act.wait_ge(setup, N_SETUP)

            def norm(n):
                act.wait_ge(ln_var, n + 1)
                act.activation(stat[:, 3, :], stat[:, 2, :], ACT.Sqrt).then_inc(ln_std, 1)

            def attention(l):
                L = lay[l]

                def body(st, par, main, prep):
                    cur = 0
                    def probabilities(c):
                        L["scores"].wait(act, st, c + 1)
                        L["pv"].wait(act, st, c + 1 - PROB)
                        s2 = 2 * (c % 2)
                        act.activation(pt[:, c % PROB, :].rearrange("p (a n) -> p a n", a=2),
                                       ps[0:CK, s2:s2 + 2, 0:HB], ACT.Exp).then_inc(L["probs"].sem, 1)

                    def units(c):
                        nonlocal cur
                        for name in plan(l, st)[c]:
                            nb = batch_of(l, par, name)[1]
                            bank = bank_of(l, st, cur)
                            cur += 1
                            k = int(name[1:] or 0)
                            if name[0] not in ACT_READS[l]:
                                continue
                            L["filled"].wait(act, st, cur)
                            if l == 1 and name[0] in "TK":
                                L["low"].wait(act, st, 2 * (low_index(name) - 1))
                            if name[0] == "T":
                                to = cTh[:, nb, KB * k:KB * k + KB] if l == 0 else full[:, low_index(name) % 2, :]
                                act.activation(to, ps[:, bank, 0:KB], ACT.Copy).then_inc(L["high"].sem, 1)
                            elif name[0] == "Q":
                                act.activation(qh[:, nb, HB * k:HB * k + HB], ps[:, bank, 0:HB],
                                               ACT.Copy).then_inc(L["high"].sem, 1)
                            elif name[0] == "V":
                                if k == 0:
                                    L["pv"].wait(act, st, 0)
                                cs = vunit(l, k)
                                n = len(cs)
                                act.activation(vx[:, nb, cs[0]:cs[-1] + 1, :, 0:2 * W],
                                               ps[0:CK, bank, 0:128 * n].rearrange("p (c q w) -> p c q w", c=n, q=NP),
                                               ACT.Copy).then_inc(L["high"].sem, 1)
                            else:
                                act.activation(full[:, low_index(name) % 2, :], ps[:, bank, 0:KB], ACT.Identity,
                                               bias=bk_s[:, 0:1]).then_inc(L["high"].sem, 1)

                    for c in range(CH):
                        first = UNITS_FIRST[l] and c == 0
                        if prep and first:
                            units(c)
                        if main:
                            probabilities(c)
                        if prep and not first:
                            units(c)

                steps(act, body, l)

            def experts(l):
                M = moe[l]
                act.wait_ge(M["lm"], 1)
                act.activation(rt[:, 2], rt[:, 1], ACT.Exp).then_inc(M["ex"], 1)

                def expert(e):
                    if l == 0:
                        if not isinstance(e, int):
                            act.wait_ge(M["act"], e * (G * NF))
                        be = b1_s[:, e, :] if isinstance(e, int) else b1_s[:, bass.ds(e, 1), :].squeeze(1)
                        act.activation(b1e[:], be, ACT.Copy).then_inc(M["bk"], 1)
                        act.wait_ge(M["bk"], e + 1)
                    for g in range(G):
                        for f in range(NF):
                            n = g * NF + f
                            act.wait_ge(M["up"], e * (G * NF) + (n + 1))
                            if f == 0 and (g > 1 or not isinstance(e, int)):
                                act.wait_ge(M["dn"], e * G + (g - 1))
                            o = hT[:, g % 2, f, :, 0:S]
                            i = ps[:, n % 4, 0:8 * S].rearrange("p (b s) -> p b s", s=S)
                            bias = b1e[:, f:f + 1] if l == 0 else zb[:, 0:1]
                            act.activation(o, i, ACT.Gelu, bias=bias).then_inc(M["act"], 1)

                expert(0)
                with act.Fori(1, E) as e:
                    expert(e)

            act.wait_ge(loaded[0], N_LOADED)
            norm(0)
            attention(0)
            norm(1)
            experts(0)
            norm(2)
            attention(1)
            norm(3)
            experts(1)

        @block.tensor
        def _(pe):
            pe.wait_ge(loaded[0], N_LOADED)
            pe.wait_ge(setup, N_SETUP)
            for h in range(H):
                mm = pe.matmul(ps[:, h // 4, 128 * (h % 4):128 * (h % 4) + 128], wqT_s[:, h, :], wkT_s[:, h, :],
                               start=True, stop=True)
                if h % 4 == 3:
                    mm.then_inc(g_ready, 1)

            def transpose_tokens(n):
                pe.wait_ge(ln_xn, n + 1)
                if n == 0:
                    pe.wait_ge(g_kept, 4)
                for i in range(NT):
                    mm = pe.transpose(ps[:, i // 4, 128 * (i % 4):128 * (i % 4) + 128], xc[:, i, :], ident[:])
                    if i % 4 == 3 or i == NT - 1:
                        mm.then_inc(xT_psum, 1)
                pe.wait_ge(xT_kept, (n + 1) * NX)

            NX = (NT + 3) // 4

            def attention(l):
                L = lay[l]

                def scores(st, par, c):
                    L["probs"].wait(pe, st, c - 1)
                    if l == 1 and c == 0:
                        wait_read(pe, l, st, "R", back=1)
                    for a in range(2):
                        cols = slice(HB * a, HB * a + HB)
                        o = ps[0:CK, 2 * (c % 2) + a, 0:HB]
                        ks = slice(CK * c, CK * c + CK)
                        if l == 0:
                            pe.matmul(o, cTh[:, par, ks], qh[:, par, cols], start=True, stop=False)
                            pe.matmul(o, cTh[:, par, ks], ql[:, par, cols], start=False, stop=False)
                            pe.matmul(o, cTl[:, par, ks], qh[:, par, cols], start=False, stop=False)
                        else:
                            for g in range(2 * a, 2 * a + 2):
                                mm = pe.matmul(ps[0:CK, 2 * (c % 2) + a, 224 * (g % 2):224 * (g % 2) + 224],
                                               kst[:, par, g, ks], qst[:, par, 224 * g:224 * g + 224],
                                               start=True, stop=True)
                    if l == 0:
                        if c == 0:
                            wait_read(pe, l, st, "R", back=1)
                        for a in range(2):
                            mm = pe.matmul(ps[0:CK, 2 * (c % 2) + a, 0:HB], ones16[:, :], sh[:, par, HB * a:HB * a + HB],
                                           start=False, stop=True)
                    mm.then_inc(L["scores"].sem, 1)

                def values(st, par, c, back):
                    L["probs"].wait(pe, st, c + 1, back=back)
                    if c == 0:
                        L["out"].wait(pe, st, L["out"].per, back=back + 1)
                    for p in range(NP):
                        j = p % 4
                        mm = pe.matmul(ps[32 * j:32 * j + 32, 7, PR * (p // 4):PR * (p // 4) + PR],
                                       vx[:, par, c, p, :], pt[:, c % PROB, PR * p:PR * p + PR],
                                       start=(c == 0 and p < 4), stop=(c == CH - 1), skip_group_check=True)
                    mm.then_inc(L["pv"].sem, 1)

                def turn_out(st, back):
                    L["o_kept"].wait(pe, st, 1, back=back)
                    base = PB * ((st.c - back) % 2)
                    for s in range(2):
                        for a in range(2):
                            n = 2 * s + a
                            mm = pe.matmul(ps[base:base + S, 7, 128 * n:128 * n + 128], o_s[:, s, S * a:S * a + S],
                                           ident[:, :], start=True, stop=True)
                    mm.then_inc(L["outT"].sem, 1)

                def unit(st, par, name, i):
                    ahead, nb = batch_of(l, par, name)
                    wait_read(pe, l, st, i - 3)
                    bank = bank_of(l, st, i)
                    k = int(name[1:] or 0)
                    if name[0] == "T":
                        if k == 0:
                            pe.wait_ge(L["ctx"][nb], (tile_index(st, ahead) + 1) * 16)
                        for q in range(4):
                            mm = pe.transpose(ps[:, bank, CK * q:CK * q + CK], cn[:, nb, 4 * k + q, :], ident[0:CK, 0:CK])
                    elif name[0] == "V":
                        if k == 0:
                            if l == 0:
                                wait_read(pe, l, st, "T2")
                            else:
                                L["low"].wait(pe, st, 2 * low_index("T2") + 2, back=1)
                        chunks = vunit(l, k)
                        for q, c in enumerate(chunks):
                            o = ps[0:CK, bank, 128 * q:128 * q + 128]
                            ks = slice(CK * c, CK * c + CK)
                            pe.matmul(o, cTh[:, nb, ks], wvh[l][:], start=True, stop=False)
                            pe.matmul(o, cTh[:, nb, ks], wvl[l][:], start=False, stop=False)
                            mm = pe.matmul(o, cTl[:, nb, ks], wvh[l][:], start=False, stop=True)
                    elif name[0] == "K":
                        L["low"].wait(pe, st, 2 * low_index(f"T{k}") + 2)
                        o = ps[:, bank, 0:KB]
                        ks = slice(KB * k, KB * k + KB)
                        pe.matmul(o, wk1h[:], cTh[:, nb, ks], start=True, stop=False)
                        pe.matmul(o, wk1h[:], cTl[:, nb, ks], start=False, stop=False)
                        mm = pe.matmul(o, wk1l[:], cTh[:, nb, ks], start=False, stop=True)
                    elif name[0] == "Q":
                        ti = tile_index(st, ahead)
                        off = PB * nb
                        if isinstance(ti, int):
                            rhs = xT[:, 128 * ti + off:128 * ti + off + S]
                        else:
                            rhs = xT[:, bass.ds(ti * 128 + off, S)]
                        if l == 0:
                            for q in range(8):
                                mm = pe.matmul(ps[:, bank, S * q:S * q + S], g_s[:, 8 * k + q, :], rhs, start=True, stop=True)
                        else:
                            for g in range(NG):
                                mm = pe.matmul(ps[0:SHIFT, bank, S * g:S * g + S],
                                               wq1r[:, g].rearrange("p r w -> p (r w)"), rhs, start=True, stop=True)
                    elif name[0] == "M":
                        p, kb = max_unit(l, k)
                        ks = slice(KB * kb, KB * kb + KB)
                        rows = slice(PR * p, PR * p + PR)
                        if l == 0:
                            if k == 0:
                                wait_read(pe, l, st, "Q1")
                            mm = pe.matmul(ps[0:PR, bank, 0:KB], qh[:, nb, rows], cTh[:, nb, ks], start=True, stop=True)
                        else:
                            if k == 0:
                                L["spread"].wait(pe, st, 1)
                            for h, (k0, k1) in enumerate(PARTS1):
                                if kb == k0 and p == 0:
                                    L["masked"][h].wait(pe, st, 0)
                                if kb == k0 and p % 2 == 0:
                                    L["stack"][h][p // 2].wait(pe, st, 0)
                            n = SHIFT + 1
                            mm = pe.matmul(ps[0:PR, bank, 0:KB], qst[0:n, nb, rows], kst[0:n, nb, p // 2, ks],
                                           start=True, stop=True)
                    else:
                        L["prep"].wait(pe, st, prep_count(l, st, "R"))
                        mm = pe.matmul(ps[SHIFT:SHIFT + NSH, bank, 0:PR], mx[:, 0:NSH], negid[:], start=True, stop=True)
                    mm.then_inc(L["filled"].sem, 1)

                def body(st, par, main, prep):
                    i = 0
                    def units(c):
                        nonlocal i
                        for name in plan(l, st)[c]:
                            unit(st, par, name, i)
                            i += 1

                    for c in range(CH):
                        first = UNITS_FIRST[l] and c == 0
                        if prep and first:
                            units(c)
                        if main:
                            scores(st, par, c)
                            for v in PV_AT[l][c]:
                                if v >= 0:
                                    values(st, par, v, 0)
                                elif st.j is not None or st.c > 0:
                                    values(st, 1 - par, CH + v, 1)
                            if c == OUT_AT and (st.j is not None or st.c > 0):
                                turn_out(st, 1)
                        if prep and not first:
                            units(c)
                    if main and not prep:
                        for c in (CH - 2, CH - 1):
                            values(st, par, c, 0)
                        turn_out(st, 0)

                steps(pe, body, l)

            def experts(l):
                M = moe[l]
                for i in range(NT):
                    mm = pe.matmul(ps[:, 7, E * i:E * i + E], xT[:, 128 * i:128 * i + 128], wr_s[l][:], start=True, stop=True)
                mm.then_inc(M["lg"], 1)
                pe.wait_ge(M["ch"], 1)
                if l == 0:
                    pe.transpose(ps[0:NT * E, 7, 0:128], gate[:].rearrange("p i e -> p (i e)"), ident[:]).then_inc(M["rp"], 1)
                    pe.wait_ge(M["gt"], 1)
                    for i in range(NT):
                        mm = pe.matmul(ps[:, i // 4, 128 * (i % 4):128 * (i % 4) + 128], gateT[0:NT * E, :], b2x[0:NT * E, i, :],
                                       start=True, stop=True)
                    mm.then_inc(M["rp"], 1)
                else:
                    for k in range(2):
                        oh = rt[:, 4 + k].rearrange("p i e -> p (i e)")
                        pe.matmul(ps[:, 7, 256 * k:256 * k + NT * E], tri[:], oh, start=True, stop=True)
                        mm = pe.matmul(ps[:, 7, 256 * k + 128:256 * k + 128 + NT * E], real[:], oh, start=True, stop=True)
                    mm.then_inc(M["rp"], 1)
                pe.wait_ge(M["rd"], 1)

                def up(e, par, g):
                    for f in range(NF):
                        n = g * NF + f
                        if n > 3 or not (isinstance(e, int) and e == 0):
                            pe.wait_ge(M["act"], e * (G * NF) + (n - 3))
                        rhs = xT[:, 512 * g:512 * g + 512].rearrange("p (b s) -> p b s", s=PB)[:, :, 0:S]
                        pe.matmul(ps[:, n % 4, 0:8 * S].rearrange("p (b s) -> p b s", s=S), up_s[:, par, 128 * f:128 * f + 128],
                                  rhs, start=True, stop=True).then_inc(M["up"], 1)

                def down(e, par, q):
                    pe.wait_ge(M["act"], e * (G * NF) + NF * (q + 1))
                    if q > 1 or not (isinstance(e, int) and e == 0):
                        pe.wait_ge(M["add"], e * G + (q - 1))
                    for t in range(4):
                        for f in range(NF):
                            lhs = hT[:, q % 2, f, 2 * t:2 * t + 2, :].rearrange("p b s -> p (b s)")
                            mm = pe.matmul(ps[:, 4 + q % 2, 128 * t:128 * t + 128], lhs, down_s[:, par, f, :],
                                           start=(f == 0), stop=(f == NF - 1))
                    mm.then_inc(M["dn"], 1)

                def expert(e, par):
                    first = isinstance(e, int) and e == 0
                    pe.wait_ge(M["wl"][par], 32 if isinstance(e, int) else e * 16 + (32 - 16 * par))
                    for g in range(G):
                        up(e, par, g)
                        if g > 0:
                            down(e, par, g - 1)
                        elif not first:
                            down(e - 1, 1 - par, G - 1)

                expert(0, 0)
                expert(1, 1)
                with pe.Fori(1, E // 2) as j:
                    expert(j * 2, 0)
                    expert(j * 2 + 1, 1)
                down(E - 1, 1, G - 1)

            transpose_tokens(0)
            attention(0)
            transpose_tokens(1)
            experts(0)
            transpose_tokens(2)
            attention(1)
            transpose_tokens(3)
            experts(1)

        @block.vector
        def _(dve):
            NX = (NT + 3) // 4
            dve.wait_ge(loaded[0], N_LOADED)
            dve.wait_ge(setup, N_SETUP)
            lns = [0]

            def link(ins):
                lns[0] += 1
                ins.then_inc(ln_step, 1)
                dve.wait_ge(ln_step, lns[0])

            for w, hi, lo in ((wv_s[0], wvh[0], wvl[0]), (wv_s[1], wvh[1], wvl[1]), (wk1_s, wk1h, wk1l)):
                link(dve.tensor_copy(hi[:], w[:]))
                link(dve.tensor_tensor(lo[:], w[:], hi[:], ALU.subtract))
            rs = float(1.0 / np.sqrt(np.float32(W)))
            for r in range(3):
                link(dve.tensor_scalar(wq1r[:, :, r, :], wq1_s[:].rearrange("p (g w) -> p g w", g=NG), rs, None, ALU.mult))
            link(dve.tensor_scalar(bqs[:], bqr_s[:], rs, None, ALU.mult))
            dve.tensor_scalar(mf[:], mi[:], -1.0, None, ALU.add).then_inc(mf_kept, 1)
            for n in range(4):
                dve.wait_ge(g_ready, n + 1)
                dve.tensor_scalar(g_s[:, 4 * n:4 * n + 4, :], ps[:, n, :].rearrange("p (h d) -> p h d", h=4),
                                  float(DK0) ** -0.5, None, ALU.mult).then_inc(g_kept, 1)
            link(dve.tensor_tensor(b2x[:], b2_s[:].unsqueeze(1).broadcast_to([128, NT, D]),
                                   selte[:].unsqueeze(2).broadcast_to([128, NT, D]), ALU.mult))

            def norm(n):
                link(dve.tensor_reduce(stat[:, 0, :], xs[:], AX.X, ALU.add))
                link(dve.tensor_scalar(stat[:, 1, :], stat[:, 0, :], 1.0 / D, None, ALU.mult))
                link(dve.tensor_tensor(xc[:], xs[:], stat[:, 1, :].unsqueeze(2).broadcast_to([128, NT, D]), ALU.subtract))
                link(dve.tensor_tensor(xsq[:], xc[:], xc[:], ALU.mult))
                link(dve.tensor_reduce(stat[:, 0, :], xsq[:], AX.X, ALU.add))
                dve.tensor_scalar(stat[:, 2, :], stat[:, 0, :], 1.0 / D, EPS, ALU.mult, ALU.add).then_inc(ln_var, 1)
                dve.wait_ge(ln_std, n + 1)
                link(dve.reciprocal(stat[:, 4, :], stat[:, 3, :]))
                link(dve.tensor_tensor(stat[:, 5, :], stat[:, 4, :], stat[:, 4, :], ALU.mult))
                link(dve.tensor_tensor(stat[:, 5, :], stat[:, 5, :], stat[:, 2, :], ALU.mult))
                link(dve.tensor_scalar(stat[:, 5, :], stat[:, 5, :], -0.5, 1.5, ALU.mult, ALU.add))
                link(dve.tensor_tensor(stat[:, 4, :], stat[:, 4, :], stat[:, 5, :], ALU.mult))
                dve.tensor_tensor(xc[:], xc[:], stat[:, 4, :].unsqueeze(2).broadcast_to([128, NT, D]),
                                  ALU.mult).then_inc(ln_xn, 1)
                for i in range(NX):
                    dve.wait_ge(xT_psum, n * NX + i + 1)
                    w = min(4, NT - 4 * i) * 128
                    dve.tensor_copy(xT[:, 512 * i:512 * i + w], ps[:, i, 0:w]).then_inc(xT_kept, 1)

            def attention(l):
                L = lay[l]

                def keep_sums(st, back):
                    L["pv"].wait(dve, st, CH, back=back)
                    dve.tensor_copy(o_s[:].rearrange("p s n -> p (s n)"), ps[:, 7, 0:2 * PR]).then_inc(L["o_kept"].sem, 1)

                def add_out(st, back):
                    base = PB * ((st.c - back) % 2)
                    rows = slice(base, base + S)
                    O = L["out"]
                    L["outT"].wait(dve, st, 1, back=back)
                    src = ps[rows, 7, :].rearrange("p (s a j w) -> p s a j w", s=2, a=2, j=NG)
                    dve.reciprocal(rden[rows], src[:, :, :, :, 2 * W]).then_inc(O.sem, 1)
                    O.wait(dve, st, 1, back=back)
                    dst = on[rows, :].rearrange("p (s j a w) -> p s a j w", s=2, j=NG, a=2)
                    for a in range(2):
                        dve.tensor_tensor(dst[:, :, a], src[:, :, a, :, W * a:W * a + W],
                                          rden[rows, :, a, :].unsqueeze(3).broadcast_to([S, 2, NG, W]),
                                          ALU.mult).then_inc(O.sem, 1)
                    k = 3
                    O.wait(dve, st, k, back=back)
                    if l == 1:
                        dve.tensor_tensor(on[rows], on[rows], bv_s[rows], ALU.add).then_inc(O.sem, 1)
                        k += 1
                        O.wait(dve, st, k, back=back)
                    ti = tile_index(st, -back)
                    xv = xs[rows, ti, :] if isinstance(ti, int) else xs[rows, bass.ds(ti, 1), :].squeeze(1)
                    dve.tensor_tensor(xv, xv, on[rows, :], ALU.add).then_inc(O.sem, 1)

                def unit(st, nb, name, i, highs):
                    F, P = L["free"], L["prep"]
                    if name[0] in ACT_RELEASES[l]:
                        return
                    L["filled"].wait(dve, st, i + 1)
                    bank = bank_of(l, st, i)
                    k = int(name[1:] or 0)
                    if name[0] == "T":
                        ks = slice(KB * k, KB * k + KB)
                        L["high"].wait(dve, st, highs)
                        dve.tensor_tensor(cTl[:, nb, ks], ps[:, bank, 0:KB], cTh[:, nb, ks], ALU.subtract).then_inc(F.sem, 1)
                    elif name[0] == "V":
                        cs = vunit(l, k)
                        n = len(cs)
                        dve.tensor_copy(vx[:, nb, cs[0]:cs[-1] + 1, :, 0:2 * W],
                                        ps[0:CK, bank, 0:128 * n].rearrange("p (c q w) -> p c q w", c=n, q=NP)).then_inc(F.sem, 1)
                    elif name[0] == "Q" and l == 0:
                        cs = slice(HB * k, HB * k + HB)
                        L["high"].wait(dve, st, highs)
                        dve.tensor_tensor(ql[:, nb, cs], ps[:, bank, 0:HB], qh[:, nb, cs], ALU.subtract).then_inc(F.sem, 1)
                    elif name[0] == "Q":
                        dve.tensor_tensor(qt[:], ps[0:SHIFT, bank, 0:NG * S].rearrange("p (g s) -> p g s", g=NG),
                                          bqs[:].unsqueeze(2).broadcast_to([SHIFT, NG, S]), ALU.add).then_inc(F.sem, 1)
                        wait_read(dve, l, st, i)
                        L["spread"].wait(dve, st, 1)
                        dve.tensor_copy(qhl[:], qt[:]).then_inc(P.sem, 1)
                        P.wait(dve, st, prep_count(l, st, name) + 1)
                        dve.tensor_tensor(qhl[2 * GW:], qt[2 * GW:], qhl[2 * GW:], ALU.subtract).then_inc(P.sem, 1)
                    elif name[0] == "M":
                        p, kb = max_unit(l, k)
                        dve.tensor_reduce(mp[:, p, kb:kb + 1], ps[0:PR, bank, 0:KB], AX.X, ALU.max).then_inc(F.sem, 1)
                        if k == 3 * NP - 1:
                            wait_read(dve, l, st, i)
                            dve.tensor_reduce(mx[:, 1:NSH], mp[:], AX.X, ALU.max).then_inc(P.sem, 1)
                    else:
                        dst = sh if l == 0 else qst
                        dve.tensor_tensor(dst[SHIFT:SHIFT + NSH, nb, :].rearrange("p (q n) -> p q n", q=NP),
                                          ps[SHIFT:SHIFT + NSH, bank, 0:PR].unsqueeze(1).broadcast_to([NSH, NP, PR]),
                                          sel[l][SHIFT:SHIFT + NSH, :].unsqueeze(2).broadcast_to([NSH, NP, PR]),
                                          ALU.mult).then_inc(F.sem, 1)

                def body(st, par, main, prep):
                    i = highs = 0
                    for c in range(CH):
                        if main and (st.j is not None or st.c > 0):
                            if c == 2:
                                keep_sums(st, 1)
                            if c == OUT_AT + 1:
                                add_out(st, 1)
                        if prep:
                            for name in plan(l, st)[c]:
                                highs += name[0] in ACT_READS[l]
                                unit(st, batch_of(l, par, name)[1], name, i, highs)
                                i += 1
                    if main and not prep:
                        keep_sums(st, 0)
                        add_out(st, 0)
                        L["out"].wait(dve, st, L["out"].per)

                steps(dve, body, l)

            def experts(l):
                M = moe[l]
                n = [0]

                def link(ins):
                    n[0] += 1
                    ins.then_inc(M["rs"], 1)
                    dve.wait_ge(M["rs"], n[0])

                def wide(a):
                    return a.unsqueeze(2).broadcast_to([128, NT, E])

                ev = eidx[:].unsqueeze(1).broadcast_to([128, NT, E])

                def first_of(dst, values, scratch, m):
                    link(dve.tensor_reduce(m, values, AX.X, ALU.max))
                    link(dve.tensor_tensor(scratch, values, wide(m), ALU.is_equal))
                    link(dve.tensor_tensor(scratch, scratch, ev, ALU.mult))
                    link(dve.tensor_reduce(m, scratch, AX.X, ALU.max))
                    link(dve.tensor_tensor(dst, scratch, wide(m), ALU.is_equal))

                lg = ps[:, 7, 0:NT * E].rearrange("p (i e) -> p i e", e=E)
                dve.wait_ge(M["lg"], 1)
                link(dve.tensor_copy(rt[:, 0], lg))
                link(dve.tensor_reduce(r1[:, 0], rt[:, 0], AX.X, ALU.max))
                dve.tensor_tensor(rt[:, 1], rt[:, 0], wide(r1[:, 0]), ALU.subtract).then_inc(M["lm"], 1)
                dve.wait_ge(M["ex"], 1)
                if l == 0:
                    first_of(rt[:, 4], rt[:, 2], rt[:, 3], r1[:, 1])
                    link(dve.tensor_reduce(r1[:, 2], rt[:, 2], AX.X, ALU.add))
                    link(dve.tensor_reduce(r1[:, 4], rt[:, 2], AX.X, ALU.max))
                    link(dve.reciprocal(r1[:, 3], r1[:, 2]))
                    link(dve.tensor_tensor(r1[:, 3], r1[:, 3], r1[:, 4], ALU.mult))
                    dve.tensor_tensor(gate[:], rt[:, 4], wide(r1[:, 3]), ALU.mult).then_inc(M["ch"], 1)
                    dve.wait_ge(M["rp"], 1)
                    dve.tensor_copy(gateT[0:NT * E, :], ps[0:NT * E, 7, 0:128]).then_inc(M["gt"], 1)
                    dve.wait_ge(M["rp"], 2)
                    for i in range(NX):
                        k = min(4, NT - 4 * i)
                        xv = xs[:, 4 * i:4 * i + k, :]
                        ins = dve.tensor_tensor(xv, xv, ps[:, i, 0:128 * k].rearrange("p (t d) -> p t d", d=D), ALU.add)
                        if i < NX - 1:
                            link(ins)
                    ins.then_inc(M["rd"], 1)
                else:
                    first_of(rt[:, 4], rt[:, 1], rt[:, 3], r1[:, 1])
                    link(dve.scalar_tensor_tensor(out=rt[:, 6], in0=rt[:, 4], scalar=-3.0e38, in1=rt[:, 1],
                                                  op0=ALU.mult, op1=ALU.add))
                    first_of(rt[:, 5], rt[:, 6], rt[:, 3], r1[:, 2])
                    link(dve.tensor_tensor(rt[:, 8], rt[:, 2], rt[:, 5], ALU.mult))
                    link(dve.tensor_reduce(r1[:, 4], rt[:, 8], AX.X, ALU.add))
                    link(dve.tensor_scalar(r1[:, 5], r1[:, 4], 1.0, None, ALU.add))
                    link(dve.reciprocal(r1[:, 6], r1[:, 5]))
                    dve.tensor_tensor(r1[:, 7], r1[:, 4], r1[:, 6], ALU.mult).then_inc(M["ch"], 1)
                    dve.wait_ge(M["rp"], 1)
                    for k in range(2):
                        pre = ps[:, 7, 256 * k:256 * k + NT * E].rearrange("p (i e) -> p i e", e=E)
                        tot = ps[:, 7, 256 * k + 128:256 * k + 128 + NT * E].rearrange("p (i e) -> p i e", e=E)
                        a, b = 8, 9
                        link(dve.tensor_copy(rt[:, a], tot))
                        d = 1
                        while d < NT:
                            link(dve.tensor_copy(rt[:, b, 0:d], rt[:, a, 0:d]))
                            link(dve.tensor_tensor(rt[:, b, d:NT], rt[:, a, d:NT], rt[:, a, 0:NT - d], ALU.add))
                            a, b, d = b, a, 2 * d
                        if k == 0:
                            link(dve.tensor_copy(rt[:, 12, 0:1], rt[:, a, NT - 1:NT]))
                        link(dve.tensor_tensor(rt[:, 10], rt[:, a], tot, ALU.subtract))
                        link(dve.tensor_tensor(rt[:, 10], rt[:, 10], pre, ALU.add))
                        if k == 1:
                            link(dve.tensor_tensor(rt[:, 10], rt[:, 10], rt[:, 12, 0:1, :].broadcast_to([128, NT, E]), ALU.add))
                        link(dve.scalar_tensor_tensor(out=rt[:, 11], in0=rt[:, 10], scalar=float(cap), in1=rt[:, 4 + k],
                                                      op0=ALU.is_lt, op1=ALU.mult))
                        link(dve.tensor_tensor(rt[:, 13 + k], rt[:, 11], wide(r1[:, 6 + k]), ALU.mult))
                    dve.tensor_tensor(gate[:], rt[:, 13], rt[:, 14], ALU.add).then_inc(M["rd"], 1)
                dve.wait_ge(M["rd"], 1)

                def expert(e):
                    for g in range(G):
                        dve.wait_ge(M["dn"], e * G + (g + 1))
                        if not isinstance(e, int):
                            dve.wait_ge(M["add"], (e - 1) * G + (g + 1))
                        bank = 4 + g % 2
                        for t in range(4):
                            i = 4 * g + t
                            ins = dve.scalar_tensor_tensor(out=xs[:, i, :], in0=ps[:, bank, 128 * t:128 * t + 128],
                                                           scalar=gate[:, i, e:e + 1] if isinstance(e, int) else gate[:, i, bass.ds(e, 1)], in1=xs[:, i, :],
                                                           op0=ALU.mult, op1=ALU.add)
                        ins.then_inc(M["add"], 1)

                expert(0)
                with dve.Fori(1, E) as e:
                    expert(e)
                dve.wait_ge(M["add"], E * G)

            norm(0)
            attention(0)
            norm(1)
            experts(0)
            norm(2)
            attention(1)
            norm(3)
            experts(1)



_IN = ["x", "ctx", "mask", "wqT", "wkT", "wv", "wr0", "w1", "b1", "w2", "b2rep", "wq1T", "bqr", "wk1T", "bk", "wv1T", "bv",
       "wg", "fc", "proj", "ident", "negid", "hmask", "sel0", "sel1", "selte", "tri", "real", "eidx"]


def constants(NT):
    p = np.arange(128)
    is_real = (p % PB) < S
    sel1 = np.zeros((128, NP), np.float32)
    for t in range(NP):
        sel1[SHIFT + 1 + t, t] = 1
    sel0 = sel1.copy()
    sel1[SHIFT] = 1
    return dict(
        ident=np.eye(128, dtype=np.float32), negid=-np.eye(PR, dtype=np.float32),
        hmask=((p[:SHIFT, None] % GW) // W == np.arange(4)).astype(np.float16), sel0=sel0, sel1=sel1,
        selte=(p[:, None] // E == np.arange(NT)).astype(np.float32),
        tri=((p[:, None] < p[None]) & is_real[:, None]).astype(np.float32),
        real=np.repeat(is_real[:, None], 128, 1).astype(np.float32),
        eidx=np.repeat((E - np.arange(E, dtype=np.float32))[None], 128, 0))


def laid_out(i):
    a = {k: np.asarray(v) for k, v in i.items()}
    B = a["x"].shape[0]
    NT = B // 2
    d = dict(
        x=a["x"], ctx=a["ctx_1024"], mask=a["mask_BxS2_ik0"], wqT=a["L0_xattn_wq"].T, wkT=a["L0_xattn_wk"].T,
        wv=a["L0_xattn_wv"], wr0=a["L0_ffn_Wr"], w1=a["L0_ffn_W1"],
        b1=a["L0_ffn_b1"].reshape(E, NF, 128).transpose(2, 0, 1),
        w2=a["L0_ffn_W2"].reshape(E, NF, 128, D).transpose(0, 2, 1, 3), b2rep=np.tile(a["L0_ffn_b2"], (128 // E, 1)),
        wq1T=a["L1_xattn_Wq"].T, bqr=np.tile(a["L1_xattn_bq"].reshape(NG, GW).T, (3, 1)), wk1T=a["L1_xattn_Wk"].T,
        bk=a["L1_xattn_bk"].reshape(D, 1), wv1T=a["L1_xattn_Wv"].T, bv=np.tile(a["L1_xattn_bv"][None], (S + PB, 1)),
        wg=a["L1_ffn_w_g"], fc=a["L1_ffn_c_fc"], proj=a["L1_ffn_c_proj"].reshape(E, NF, 128, D).transpose(0, 2, 1, 3))
    d.update(constants(NT))
    return B, {k: np.ascontiguousarray(v) for k, v in d.items()}


def kernel(**inputs):
    import concourse.bacc as bacc
    from concourse.bass_utils import run_bass_kernel_spmd

    B, arrays = laid_out(inputs)
    nc = bacc.Bacc("TRN2", target_bir_lowering=False, num_devices=1)
    arrays = {"in_" + n: a for n, a in arrays.items()}
    args = [nc.dram_tensor(n, arrays[n].shape, mybir.dt.from_np(arrays[n].dtype), kind="ExternalInput").ap() for n in ("in_" + n for n in _IN)]
    out = nc.dram_tensor("out", [B, S, D], F32, kind="ExternalOutput").ap()
    program(nc, B, args, out)
    r = run_bass_kernel_spmd(nc, [arrays], core_ids=[0])
    return r.results[0]["out"]
```

```python
from contextlib import ExitStack

import numpy as np

import concourse.bass as bass
from concourse import mybir

F32 = mybir.dt.float32
F16 = mybir.dt.float16
I32 = mybir.dt.int32
ALU = mybir.AluOpType
ACT = mybir.ActivationFunctionType
AX = mybir.AxisListType

S, D = 56, 128
NK, CH = 1500, 12
CK = NK // CH
H = 16
DK0 = 64
W = D // H
NP = H // 2
PR = 2 * S
NG = 4
GW = D // NG
COLS = H * S
HB = COLS // 2
BANK = 512
KB = 500
NKB = NK // KB
PB = 64
E, FF = 8, 512
NF = FF // 128
SHIFT = 96
NSH = 1 + NP
WS = 64.0
TOPM = 10000.0
PROB = 6
EPS = 1e-5

def numbered(text):
    m, out = 0, []
    for chunk in text.split("|"):
        out.append([])
        for name in chunk.split():
            if name == "M":
                name, m = f"M{m}", m + 1
            out[-1].append(name)
    assert m == NP * NKB and len(out) == CH
    return out


UNITS0 = numbered("T0 T1 | T2 Q0 | Q1 V0 | V1 M M | V2 M M | M M M | M M M | M M M | M M M | M M M M | M M M M | R")
UNITS1 = numbered("T0 M T1 | M V0 M V1 | M T2 M | K0 M M | V2 M M V3 | K1 M M | M Q0 M M | M K2 M | M M M | M M M | M M | R")
UNITS_FIRST = [False, True]
AHEAD1 = "TKQ"
FIRST1 = [[n for n in c if n[0] in AHEAD1] for c in UNITS1]
LAST1 = [[n for n in c if n[0] not in AHEAD1] for c in UNITS1]
ACT_READS = ["TQV", "TKV"]
ACT_RELEASES = ["V", "TKV"]
PARTS1 = [(0, 2), (2, 3)]
PART_AT = [k0 for k0, k1 in PARTS1]


def max_unit(l, k):
    if l == 0:
        return divmod(k, NKB)
    n = PARTS1[0][1]
    return divmod(k, n) if k < n * NP else (k - n * NP, n)


PV_AT = [[[-2], [-1], [], [], [0], [1, 2], [3, 4], [5], [6], [7], [8], [9]],
         [[-2], [-1], [], [], [], [0, 1], [2], [3, 4], [5], [6, 7], [8], [9]]]
OUT_AT = 3


class Step:

    def __init__(self, j, c):
        self.j, self.c = j, c

    def value(self, per, k, back=0):
        c = (self.c - back) * per + k
        return c if self.j is None else self.j * (2 * per) + c


class Signal:

    def __init__(self, sem, per, first, lead=0):
        self.sem, self.per, self.first, self.lead = sem, per, first, lead

    def wait(self, eng, st, k, back=0):
        if st.j is None and st.c - back < self.first:
            v = k if st.c - back == self.first - 1 and self.lead else 0
        else:
            v = self.lead + st.value(self.per, k, back + self.first)
        if st.j is not None or v > 0:
            eng.wait_ge(self.sem, v)


def program(nc, B, args, out):
    (x, ctx_d, mask, wqT, wkT, wv, wr0, w1, b1, w2, b2rep, wq1T, bqr, wk1T, bk, wv1T, bv, wg, fc,
     proj, ident_d, negid_d, hmask_d, sel0_d, sel1_d, selte_d, tri_d, real_d, eidx_d) = args
    NT = B // 2
    TOK = NT * 128
    G = B // 8
    T = B * S
    cap = int(2 * 1.25 * T / E)
    cap += cap % 2
    assert B % 8 == 0

    with ExitStack() as es:
        def sb(name, shape, dt=F32):
            return es.enter_context(nc.sbuf_tensor(name, shape, dt))

        def sem(name):
            return es.enter_context(nc.semaphore(name))

        mask16 = nc.dram_tensor("mask16", [B, NK], F16, kind="Internal").ap()
        ps = es.enter_context(nc.psum_tensor("ps", [128, 8, BANK], F32))

        ident = sb("ident", [128, 128])
        negid = sb("negid", [PR, PR])
        hmask = sb("hmask", [SHIFT, 4], F16)
        sel = [sb(f"sel{l}", [128, NP]) for l in range(2)]
        selte = sb("selte", [128, NT])
        tri = sb("tri", [128, 128])
        real = sb("real", [128, 128])
        eidx = sb("eidx", [128, E])
        ones16 = sb("ones16", [128, CK], F16)
        xsq_full = sb("xsq", [128, max(NT, H), D])
        xsq = xsq_full[:, 0:NT, :]
        b2x_full = sb("b2x", [128, max(NT, H), D])
        b2x = b2x_full[:, 0:NT, :]
        xTh, xTl = [xsq_full[:].rearrange("p h d -> p (h d)").bitcast(F16)[:, TOK * i:TOK * i + TOK] for i in range(2)]
        wqT_s = xsq_full[0:DK0, 0:H, :]
        wkT_s = b2x_full[0:DK0, 0:H, :]
        halves = sb("halves", [D, 2 * H * D], F16)[:]
        gh, gl = [halves[:, H * D * i:H * D * i + H * D] for i in range(2)]
        uph, upl, dnh, dnl = [halves[:, 2 * FF * i:2 * FF * i + 2 * FF] for i in range(4)]
        uph, upl = [a.rearrange("p (b f) -> p b f", b=2) for a in (uph, upl)]
        dnh, dnl = [a.rearrange("p (b f d) -> p b f d", b=2, d=D) for a in (dnh, dnl)]
        wv_s = [sb(f"wv{l}", [D, D]) for l in range(2)]
        wvh = [sb(f"wvh{l}", [D, D], F16) for l in range(2)]
        wvl = [sb(f"wvl{l}", [D, D], F16) for l in range(2)]
        wk1_s = sb("wk1_s", [D, D])
        wk1h = sb("wk1h", [D, D], F16)
        wk1l = sb("wk1l", [D, D], F16)
        wq1_s = sb("wq1_s", [D, D])
        wq1r = sb("wq1r", [D, NG, 3, GW])
        bqr_s = sb("bqr_s", [SHIFT, NG])
        bqs = sb("bqs", [SHIFT, NG])
        bk_s = sb("bk_s", [D, 1])
        bv_s = sb("bv_s", [S + PB, D])
        wr_s = [sb(f"wr{l}", [D, E]) for l in range(2)]
        wrh = [sb(f"wrh{l}", [D, E], F16) for l in range(2)]
        wrl = [sb(f"wrl{l}", [D, E], F16) for l in range(2)]
        b1_s = sb("b1_s", [128, E, NF])
        b1e = sb("b1e", [128, NF])
        b2_s = sb("b2_s", [128, D])
        up_s = sb("up_s", [D, 2, FF])
        down_s = sb("down_s", [128, 2, NF, D])
        xs = sb("xs", [128, NT, D])
        xc = sb("xc", [128, NT, D])
        xT = sb("xT", [D, TOK])
        stat = sb("stat", [128, 8, NT])
        cn = sb("cn", [CK, 2, CH, D])
        cTh = sb("cTh", [D, 2, NK], F16)
        cTl = sb("cTl", [D, 2, NK], F16)
        vx = sb("vx", [CK, 2, CH, NP, 32])
        qh = sb("qh", [D, 2, COLS], F16)
        ql = sb("ql", [D, 2, COLS], F16)
        h32 = [t[:, i, :].bitcast(F32) for t in (qh, ql) for i in range(2)]
        sh = sb("sh", [128, 2, COLS], F16)
        kh = sb("kh", [D, NK], F16)
        kl = sb("kl", [D, NK], F16)
        kst = sb("kst", [128, 2, NG, NK], F16)
        qst = sb("qst", [128, 2, COLS], F16)
        full = sb("full", [128, 2, KB])
        qt = sb("qt", [SHIFT, NG, S])
        qhl = sb("qhl", [SHIFT, NG, S], F16)
        mf = sb("mf", [B, NK], F16)
        mp = sb("mp", [PR, NP, NKB])
        mx = sb("mx", [PR, 32])
        ring = sb("ring", [128, PROB * COLS])
        pt = ring[0:CK, :].rearrange("p (r n) -> p r n", r=PROB)
        rt = ring[:, 0:16 * NT * E].rearrange("p (k i e) -> p k i e", k=16, e=E)
        mi = ring[0:B, 0:NK].bitcast(I32)
        o_s = sb("o_s", [128, 2, PR])
        rden = sb("rden", [128, 2, 2, NG])
        on = sb("on", [128, D])
        hTh = sb("hTh", [128, 2, NF, 8, PB], F16)
        hTl = sb("hTl", [128, 2, NF, 8, PB], F16)
        gate_s = sb("gate_s", [128, NT, E])
        gate = sb("gate", [128, NT, E])
        gateT = sb("gateT", [128, 128])
        zb = sb("zb", [128, 1])
        r1 = sb("r1", [128, 8, NT])

        loaded = [sem(f"loaded{i}") for i in range(2)]
        ready0 = sem("ready0")
        setup = sem("setup")
        g_ready = sem("g_ready")
        g_kept = sem("g_kept")
        ln_step = sem("ln_step")
        ln_var = sem("ln_var")
        ln_std = sem("ln_std")
        ln_xn = sem("ln_xn")
        xT_psum = sem("xT_psum")
        xT_kept = sem("xT_kept")
        stored = sem("stored")
        xh_kept = sem("xh_kept")
        xl_kept = sem("xl_kept")
        mf_kept = sem("mf_kept")
        mask_stored = sem("mask_stored")

        def act_signals(l, name):
            return (name[0] in ACT_READS[l]) 

        lay = []
        for l in range(2):
            u = UNITS0 if l == 0 else UNITS1
            n_units = sum(map(len, u))
            assert n_units % 3 == 0
            names = [name for c in u for name in c]
            n_high = sum(act_signals(l, name) for name in names)
            n_free = sum(name[0] not in ACT_RELEASES[l] for name in names)
            ahead = [name for c in FIRST1 for name in c] if l == 1 else []
            lay.append(dict(
                n=n_units,
                ctx=[sem(f"ctx_loaded{l}{p}") for p in range(2)],
                filled=Signal(sem(f"unit_filled{l}"), n_units, -1, len(ahead)),
                free=Signal(sem(f"unit_free{l}"), n_free, -1, sum(name[0] not in ACT_RELEASES[l] for name in ahead)),
                high=Signal(sem(f"high_kept{l}"), n_high, -1, sum(act_signals(l, name) for name in ahead)),
                low=Signal(sem(f"low_kept{l}"), 12, -1, 12),
                prep=Signal(sem(f"prep_step{l}"), 1 + 2 * l, -1, 2 * l),
                scores=Signal(sem(f"scores_ready{l}"), CH, 0),
                probs=Signal(sem(f"probs_ready{l}"), CH, 0),
                pv=Signal(sem(f"pv_done{l}"), CH, 0),
                stack=[[Signal(sem(f"keys_stacked{l}{h}{g}"), 16 * 3, -2) for g in range(NG)] for h in range(2)],
                masked=[Signal(sem(f"mask_row_loaded{l}{h}"), 16, -2) for h in range(2)],
                spread=Signal(sem(f"queries_spread{l}"), 1, -1),
                o_kept=Signal(sem(f"o_kept{l}"), 1, 0),
                outT=Signal(sem(f"outT_ready{l}"), 1, 0),
                out=Signal(sem(f"out_step{l}"), 4 + l, 0),
            ))
        moe = []
        for l in range(2):
            moe.append(dict(
                sp=sem(f"weights_split{l}"), hi=sem(f"hidden_high{l}"), lo=sem(f"hidden_split{l}"),
                wl=[sem(f"expert_loaded{l}{p}") for p in range(2)], up=sem(f"up_ready{l}"), act=sem(f"gelu_ready{l}"),
                dn=sem(f"down_ready{l}"), add=sem(f"down_added{l}"), lg=sem(f"logits_ready{l}"),
                rs=sem(f"route_step{l}"), lm=sem(f"logits_shifted{l}"), ex=sem(f"route_exp{l}"),
                ch=sem(f"choices_made{l}"), rp=sem(f"route_psum{l}"), bk=sem(f"bias_kept{l}"), gt=sem(f"gates_turned{l}"), rd=sem(f"routing_read{l}")))

        def plan(l, st, back=0):
            if l == 0:
                return UNITS0
            if st.j is None and st.c - back == -2:
                return FIRST1
            if st.j is None and st.c - back == B - 2:
                return LAST1
            return UNITS1

        def names_of(l, st, back=0):
            return [name for c in plan(l, st, back) for name in c]

        def index(l, st, name, back=0):
            return names_of(l, st, back).index(name)

        def batch_of(l, par, name):
            return (2, par) if l == 1 and name[0] in AHEAD1 else (1, 1 - par)

        def prep_count(l, st, name, back=0):
            before = names_of(l, st, back)
            before = before[:before.index(name)]
            return 2 * l * ("Q0" in before) + (f"M{NP * NKB - 1}" in before)

        def bank_of(l, st, i):
            return 4 + (i - len(names_of(l, st)) % 3 if plan(l, st) is FIRST1 else i) % 3

        def wait_read(eng, l, st, i, back=0):
            L = lay[l]
            if isinstance(i, int) and i < 0:
                back += 1
                if st.j is None and st.c - back < (-1 if l == 0 else -2):
                    return
                i += len(names_of(l, st, back))
            names = names_of(l, st, back)
            if isinstance(i, str):
                i = names.index(i)
            by_act = names[i][0] in ACT_RELEASES[l]
            k = sum(act_signals(l, name) if by_act else (name[0] not in ACT_RELEASES[l]) for name in names[:i + 1])
            L["high" if by_act else "free"].wait(eng, st, k, back)

        def low_index(name):
            return "T0 T1 T2 K0 K1 K2".split().index(name)

        def steps(eng, body, l):
            if l == 1:
                body(Step(None, -2), 0, False, True)
            body(Step(None, -1), 1, False, True)
            body(Step(None, 0), 0, True, True)
            body(Step(None, 1), 1, True, True)
            if NT > 2:
                with eng.Fori(1, NT - 1) as j:
                    body(Step(j, 0), 0, True, True)
                    body(Step(j, 1), 1, True, True)
            body(Step(None, B - 2), 0, True, True)
            body(Step(None, B - 1), 1, True, False)

        def tile_index(st, ahead):
            c = st.c + ahead
            return c // 2 if st.j is None else st.j + c // 2

        def vunit(l, k):
            n = 4 if l == 0 else 3
            return range(n * k, n * k + n)

        block = es.enter_context(nc.Block())

        N_LOADED = 16 * 25
        N_SETUP0, N_SETUP = 7, 12

        @block.sync
        def _(sp):
            sp.wait_ge(ready0, 1)
            n0 = [0]

            def first(dst, src):
                n0[0] += 1
                sp.dma_start(dst, src).then_inc(loaded[0], 16)

            for p in range(2):
                first(xs[PB * p:PB * p + S, :, :], x.rearrange("(i p) s d -> p s i d", p=2)[p])
            first(ident[:], ident_d)
            first(wqT_s[:], wqT.rearrange("(h k) d -> k h d", k=DK0))
            first(wkT_s[:], wkT.rearrange("(h k) d -> k h d", k=DK0))
            first(wv_s[0][:], wv)
            for dst, src in ((negid, negid_d), (hmask, hmask_d), (sel[0], sel0_d), (sel[1], sel1_d),
                             (selte, selte_d), (tri, tri_d), (real, real_d), (eidx, eidx_d), (wr_s[0], wr0),
                             (b1_s, b1), (b2_s, b2rep), (wk1_s, wk1T), (wq1_s, wq1T), (bqr_s, bqr),
                             (bk_s, bk), (bv_s, bv), (wv_s[1], wv1T), (wr_s[1], wg), (mi, mask)):
                first(dst[:], src)

            def attention(l):
                L = lay[l]

                def load(st, ahead, par):
                    b = st.c + ahead if st.j is None else st.j * 2 + (st.c + ahead)
                    src = ctx_d[b] if st.j is None else ctx_d[bass.ds(b, 1)].squeeze(0)
                    sp.dma_start(cn[:, par], src.rearrange("(c p) d -> p c d", p=CK)).then_inc(L["ctx"][par], 16)

                def body(st, par):
                    far = 3 + l
                    to = 1 - par if l == 0 else par
                    if st.j is not None or st.c + far < B:
                        L["filled"].wait(sp, st, index(l, st, "T2") + 1)
                        load(st, far, to)
                    if l == 1:
                        b = st.c + 2 if st.j is None else st.j * 2 + (st.c + 2)
                        for h, (k0, k1) in enumerate(PARTS1):
                            ks = slice(KB * k0, KB * k1)
                            row = mask16[b:b + 1, ks] if st.j is None else mask16[bass.ds(b, 1), ks]
                            L["scores"].wait(sp, st, KB * k1 // CK)
                            if st.j is None and st.c == -1:
                                L["filled"].wait(sp, st, index(l, st, f"M{NP * NKB - 1}") + 1)
                            sp.dma_start(kst[SHIFT:SHIFT + 1, par, :, ks],
                                         row.unsqueeze(1).broadcast_to([1, NG, KB * (k1 - k0)])).then_inc(L["masked"][h].sem, 16)
                            L["low"].wait(sp, st, 2 * low_index(f"K{k1 - 1}") + 2)
                            for g in range(NG):
                                for r, src in ((0, kh), (1, kl), (2, kh)):
                                    sp.dma_start(kst[GW * r:GW * r + GW, par, g, ks],
                                                 src[GW * g:GW * g + GW, ks]).then_inc(L["stack"][h][g].sem, 16)

                load(Step(None, 0), 0, 0)
                load(Step(None, 0), 1, 1)
                for s in range(-1 - l, 2):
                    body(Step(None, s), s % 2)
                if NT > 3:
                    with sp.Fori(1, NT - 2) as j:
                        body(Step(j, 0), 0)
                        body(Step(j, 1), 1)
                for s in range(B - 4, B - 3 + l):
                    body(Step(None, s), s % 2)

            def experts(l, up_d, down_d):
                M = moe[l]

                def load(e, p):
                    if isinstance(e, int):
                        a, b = up_d[e], down_d[e]
                    else:
                        a, b = up_d[bass.ds(e, 1)].squeeze(0), down_d[bass.ds(e, 1)].squeeze(0)
                    sp.dma_start(up_s[:, p], a).then_inc(M["wl"][p], 16)
                    sp.dma_start(down_s[:, p], b).then_inc(M["wl"][p], 16)

                load(0, 0)
                load(1, 1)
                with sp.Fori(1, E // 2) as j:
                    for p in range(2):
                        sp.wait_ge(M["sp"], (j * 2 + (p - 1)) * 6)
                        load(j * 2 + p, p)

            attention(0)
            sp.wait_ge(mf_kept, 1)
            sp.dma_start(mask16, mf[:]).then_inc(mask_stored, 16)
            sp.wait_ge(mask_stored, 16)
            experts(0, w1, w2)
            attention(1)
            experts(1, fc, proj)
            sp.wait_ge(moe[1]["add"], E * G)
            for p in range(2):
                sp.dma_start(out.rearrange("(i p) s d -> p s i d", p=2)[p], xs[PB * p:PB * p + S, :, :]).then_inc(stored, 16)
            sp.wait_ge(stored, 32)

        @block.gpsimd
        def _(pool):
            pool.memset(xs[:], 0.0).then_inc(ready0, 1)
            pool.wait_ge(ready0, 1)
            fills = [(vx[:], 0.0), (vx[:, 0, :, :, 2 * W:2 * W + 1], 1.0), (vx[:, 1, :, :, 2 * W:2 * W + 1], 1.0),
                     (ones16[:], 1.0), (sh[:], 0.0), (mx[:], -TOPM), (zb[:], 0.0),
                     (hTh[:], 0.0), (hTl[:], 0.0), (qst[SHIFT:128], 0.0), (qst[SHIFT:SHIFT + 1], TOPM), (kst[SHIFT:128], 1.0)]
            assert len(fills) == N_SETUP
            for n, (tile, value) in enumerate(fills):
                if n:
                    pool.wait_ge(setup, n)
                pool.memset(tile, value).then_inc(setup, 1)

            L = lay[1]

            def body(st, par, main, prep):
                if not prep:
                    return
                names = names_of(1, st)
                if "R" in names:
                    nb = 1 - par
                    L["scores"].wait(pool, st, 0)
                    L["prep"].wait(pool, st, prep_count(1, st, "Q0", 1) + 2, back=1)
                    pool.tensor_tensor(qst[0:SHIFT, nb, :].rearrange("p (g i s) -> p g i s", g=NG, i=4),
                                       qhl[:].unsqueeze(2).broadcast_to([SHIFT, NG, 4, S]),
                                       hmask[:].unsqueeze(1).unsqueeze(3).broadcast_to([SHIFT, NG, 4, S]),
                                       ALU.mult).then_inc(L["spread"].sem, 1)
                copies = 0
                for name in names:
                    copies += act_signals(1, name)
                    if name[0] in "TK":
                        k, n = int(name[1]), low_index(name)
                        ks = slice(KB * k, KB * k + KB)
                        hi, lo = (cTh[:, par, ks], cTl[:, par, ks]) if name[0] == "T" else (kh[:, ks], kl[:, ks])
                        if name[0] == "K" and k in PART_AT:
                            for g in range(NG):
                                L["stack"][PART_AT.index(k)][g].wait(pool, st, 0)
                        L["high"].wait(pool, st, copies)
                        pool.tensor_tensor(hi, full[:, n % 2, :], zb[:].broadcast_to([128, KB]), ALU.add).then_inc(L["low"].sem, 1)
                        L["low"].wait(pool, st, 2 * n + 1)
                        pool.tensor_tensor(lo, full[:, n % 2, :], hi, ALU.subtract).then_inc(L["low"].sem, 1)

            pool.wait_ge(loaded[0], N_LOADED)
            pool.wait_ge(setup, N_SETUP)
            def experts(l):
                M = moe[l]

                def expert(e):
                    for g in range(G):
                        for f in range(NF):
                            pool.wait_ge(M["hi"], e * (G * NF) + (g * NF + f + 1))
                            if f == 0 and (g > 1 or not isinstance(e, int)):
                                pool.wait_ge(M["dn"], e * G + (g - 1))
                            pool.tensor_tensor(hTl[:, g % 2, f, :, 0:S], h32[f].rearrange("p (b s) -> p b s", s=S),
                                               hTh[:, g % 2, f, :, 0:S], ALU.subtract).then_inc(M["lo"], 1)

                expert(0)
                with pool.Fori(1, E) as e:
                    expert(e)

            experts(0)
            steps(pool, body, 1)
            experts(1)

        @block.scalar
        def _(act):
            act.wait_ge(setup, N_SETUP0)

            def norm(n):
                act.wait_ge(ln_var, n + 1)
                act.activation(stat[:, 3, :], stat[:, 2, :], ACT.Sqrt).then_inc(ln_std, 1)
                for i in range(G):
                    act.wait_ge(xT_psum, n * G + i + 1)
                    ts = slice(512 * i, 512 * i + 512)
                    act.activation(xT[:, ts], ps[:, i, :], ACT.Copy).then_inc(xT_kept, 1)
                    act.activation(xTh[:, ts], ps[:, i, :], ACT.Copy).then_inc(xh_kept, 1)

            def attention(l):
                L = lay[l]

                def body(st, par, main, prep):
                    cur = 0
                    def probabilities(c):
                        L["scores"].wait(act, st, c + 1)
                        L["pv"].wait(act, st, c + 1 - PROB)
                        s2 = 2 * (c % 2)
                        act.activation(pt[:, c % PROB, :].rearrange("p (a n) -> p a n", a=2),
                                       ps[0:CK, s2:s2 + 2, 0:HB], ACT.Exp).then_inc(L["probs"].sem, 1)

                    def units(c):
                        nonlocal cur
                        for name in plan(l, st)[c]:
                            nb = batch_of(l, par, name)[1]
                            bank = bank_of(l, st, cur)
                            cur += 1
                            k = int(name[1:] or 0)
                            if name[0] not in ACT_READS[l]:
                                continue
                            L["filled"].wait(act, st, cur)
                            if l == 1 and name[0] in "TK":
                                L["low"].wait(act, st, 2 * (low_index(name) - 1))
                            if name[0] == "T":
                                to = cTh[:, nb, KB * k:KB * k + KB] if l == 0 else full[:, low_index(name) % 2, :]
                                act.activation(to, ps[:, bank, 0:KB], ACT.Copy).then_inc(L["high"].sem, 1)
                            elif name[0] == "Q":
                                act.activation(qh[:, nb, HB * k:HB * k + HB], ps[:, bank, 0:HB],
                                               ACT.Copy, scale=1.0 / WS).then_inc(L["high"].sem, 1)
                            elif name[0] == "V":
                                if k == 0:
                                    L["pv"].wait(act, st, 0)
                                cs = vunit(l, k)
                                n = len(cs)
                                act.activation(vx[:, nb, cs[0]:cs[-1] + 1, :, 0:2 * W],
                                               ps[0:CK, bank, 0:128 * n].rearrange("p (c q w) -> p c q w", c=n, q=NP),
                                               ACT.Copy).then_inc(L["high"].sem, 1)
                            else:
                                act.activation(full[:, low_index(name) % 2, :], ps[:, bank, 0:KB], ACT.Identity,
                                               bias=bk_s[:, 0:1]).then_inc(L["high"].sem, 1)

                    for c in range(CH):
                        first = UNITS_FIRST[l] and c == 0
                        if prep and first:
                            units(c)
                        if main:
                            probabilities(c)
                        if prep and not first:
                            units(c)
                steps(act, body, l)

            def experts(l):
                M = moe[l]
                if l == 0:
                    act.wait_ge(setup, N_SETUP)
                act.wait_ge(M["lm"], 1)
                act.activation(rt[:, 2], rt[:, 1], ACT.Exp).then_inc(M["ex"], 1)

                def expert(e):
                    if l == 0:
                        if not isinstance(e, int):
                            act.wait_ge(M["act"], e * (G * NF))
                        be = b1_s[:, e, :] if isinstance(e, int) else b1_s[:, bass.ds(e, 1), :].squeeze(1)
                        act.activation(b1e[:], be, ACT.Copy).then_inc(M["bk"], 1)
                        act.wait_ge(M["bk"], e + 1)
                    for g in range(G):
                        for f in range(NF):
                            n = g * NF + f
                            act.wait_ge(M["up"], e * (G * NF) + (n + 1))
                            if g > 0 or not isinstance(e, int):
                                act.wait_ge(M["lo"], e * (G * NF) + (n + 1 - NF))
                            i = ps[:, n % 4, 0:8 * S]
                            bias = b1e[:, f:f + 1] if l == 0 else zb[:, 0:1]
                            act.activation(h32[f], i, ACT.Gelu, bias=bias, scale=1.0 / WS).then_inc(M["act"], 1)
                            if f == 0 and (g > 1 or not isinstance(e, int)):
                                act.wait_ge(M["dn"], e * G + (g - 1))
                            act.wait_ge(M["act"], e * (G * NF) + (n + 1))
                            act.activation(hTh[:, g % 2, f, :, 0:S], h32[f].rearrange("p (b s) -> p b s", s=S),
                                           ACT.Copy).then_inc(M["hi"], 1)

                expert(0)
                with act.Fori(1, E) as e:
                    expert(e)

            act.wait_ge(loaded[0], N_LOADED)
            norm(0)
            attention(0)
            norm(1)
            experts(0)
            norm(2)
            attention(1)
            norm(3)
            experts(1)

        @block.tensor
        def _(pe):
            pe.wait_ge(loaded[0], N_LOADED)
            pe.wait_ge(setup, N_SETUP0)
            for h in range(H):
                mm = pe.matmul(ps[:, h // 4, 128 * (h % 4):128 * (h % 4) + 128], wqT_s[:, h, :], wkT_s[:, h, :],
                               start=True, stop=True)
                if h % 4 == 3:
                    mm.then_inc(g_ready, 1)

            def transpose_tokens(n):
                pe.wait_ge(ln_xn, n + 1)
                if n == 0:
                    pe.wait_ge(g_kept, 4)
                for i in range(NT):
                    mm = pe.transpose(ps[:, i // 4, 128 * (i % 4):128 * (i % 4) + 128], xc[:, i, :], ident[:])
                    if i % 4 == 3 or i == NT - 1:
                        mm.then_inc(xT_psum, 1)
                pe.wait_ge(xT_kept, (n + 1) * NX)
                pe.wait_ge(xl_kept, n + 1)

            NX = (NT + 3) // 4

            def attention(l):
                L = lay[l]

                def scores(st, par, c):
                    L["probs"].wait(pe, st, c - 1)
                    if l == 1 and c == 0:
                        wait_read(pe, l, st, "R", back=1)
                    for a in range(2):
                        cols = slice(HB * a, HB * a + HB)
                        o = ps[0:CK, 2 * (c % 2) + a, 0:HB]
                        ks = slice(CK * c, CK * c + CK)
                        if l == 0:
                            pe.matmul(o, cTh[:, par, ks], qh[:, par, cols], start=True, stop=False)
                            pe.matmul(o, cTh[:, par, ks], ql[:, par, cols], start=False, stop=False)
                            mm = pe.matmul(o, cTl[:, par, ks], qh[:, par, cols], start=False, stop=False)
                        else:
                            for g in range(2 * a, 2 * a + 2):
                                mm = pe.matmul(ps[0:CK, 2 * (c % 2) + a, 224 * (g % 2):224 * (g % 2) + 224],
                                               kst[:, par, g, ks], qst[:, par, 224 * g:224 * g + 224],
                                               start=True, stop=True)
                    if l == 0:
                        if c == 0:
                            wait_read(pe, l, st, "R", back=1)
                        for a in range(2):
                            mm = pe.matmul(ps[0:CK, 2 * (c % 2) + a, 0:HB], ones16[:, :], sh[:, par, HB * a:HB * a + HB],
                                           start=False, stop=True)
                    mm.then_inc(L["scores"].sem, 1)

                def values(st, par, c, back):
                    L["probs"].wait(pe, st, c + 1, back=back)
                    if c == 0:
                        L["out"].wait(pe, st, L["out"].per, back=back + 1)
                    for p in range(NP):
                        j = p % 4
                        mm = pe.matmul(ps[32 * j:32 * j + 32, 7, PR * (p // 4):PR * (p // 4) + PR],
                                       vx[:, par, c, p, :], pt[:, c % PROB, PR * p:PR * p + PR],
                                       start=(c == 0 and p < 4), stop=(c == CH - 1), skip_group_check=True)
                    mm.then_inc(L["pv"].sem, 1)

                def turn_out(st, back):
                    L["o_kept"].wait(pe, st, 1, back=back)
                    base = PB * ((st.c - back) % 2)
                    for s in range(2):
                        for a in range(2):
                            n = 2 * s + a
                            mm = pe.matmul(ps[base:base + S, 7, 128 * n:128 * n + 128], o_s[:, s, S * a:S * a + S],
                                           ident[:, :], start=True, stop=True)
                    mm.then_inc(L["outT"].sem, 1)

                def unit(st, par, name, i):
                    ahead, nb = batch_of(l, par, name)
                    wait_read(pe, l, st, i - 3)
                    bank = bank_of(l, st, i)
                    k = int(name[1:] or 0)
                    if name[0] == "T":
                        if k == 0:
                            pe.wait_ge(L["ctx"][nb], (tile_index(st, ahead) + 1) * 16)
                        for q in range(4):
                            mm = pe.transpose(ps[:, bank, CK * q:CK * q + CK], cn[:, nb, 4 * k + q, :], ident[0:CK, 0:CK])
                    elif name[0] == "V":
                        if k == 0:
                            if l == 0:
                                wait_read(pe, l, st, "T2")
                            else:
                                L["low"].wait(pe, st, 2 * low_index("T2") + 2, back=1)
                        chunks = vunit(l, k)
                        for q, c in enumerate(chunks):
                            o = ps[0:CK, bank, 128 * q:128 * q + 128]
                            ks = slice(CK * c, CK * c + CK)
                            pe.matmul(o, cTh[:, nb, ks], wvh[l][:], start=True, stop=False)
                            pe.matmul(o, cTh[:, nb, ks], wvl[l][:], start=False, stop=False)
                            mm = pe.matmul(o, cTl[:, nb, ks], wvh[l][:], start=False, stop=True)
                    elif name[0] == "K":
                        L["low"].wait(pe, st, 2 * low_index(f"T{k}") + 2)
                        o = ps[:, bank, 0:KB]
                        ks = slice(KB * k, KB * k + KB)
                        pe.matmul(o, wk1h[:], cTh[:, nb, ks], start=True, stop=False)
                        pe.matmul(o, wk1h[:], cTl[:, nb, ks], start=False, stop=False)
                        mm = pe.matmul(o, wk1l[:], cTh[:, nb, ks], start=False, stop=True)
                    elif name[0] == "Q":
                        ti = tile_index(st, ahead)
                        off = PB * nb
                        if isinstance(ti, int):
                            rhs, xh, xl = [t[:, 128 * ti + off:128 * ti + off + S] for t in (xT, xTh, xTl)]
                        else:
                            rhs, xh, xl = [t[:, bass.ds(ti * 128 + off, S)] for t in (xT, xTh, xTl)]
                        if l == 0:
                            for q in range(8):
                                o = ps[:, bank, S * q:S * q + S]
                                gs = slice(D * (8 * k + q), D * (8 * k + q) + D)
                                pe.matmul(o, gh[:, gs], xh, start=True, stop=False)
                                pe.matmul(o, gh[:, gs], xl, start=False, stop=False)
                                mm = pe.matmul(o, gl[:, gs], xh, start=False, stop=True)
                        else:
                            for g in range(NG):
                                mm = pe.matmul(ps[0:SHIFT, bank, S * g:S * g + S],
                                               wq1r[:, g].rearrange("p r w -> p (r w)"), rhs, start=True, stop=True)
                    elif name[0] == "M":
                        p, kb = max_unit(l, k)
                        ks = slice(KB * kb, KB * kb + KB)
                        rows = slice(PR * p, PR * p + PR)
                        if l == 0:
                            if k == 0:
                                wait_read(pe, l, st, "Q1")
                            mm = pe.matmul(ps[0:PR, bank, 0:KB], qh[:, nb, rows], cTh[:, nb, ks], start=True, stop=True)
                        else:
                            if k == 0:
                                L["spread"].wait(pe, st, 1)
                            for h, (k0, k1) in enumerate(PARTS1):
                                if kb == k0 and p == 0:
                                    L["masked"][h].wait(pe, st, 0)
                                if kb == k0 and p % 2 == 0:
                                    L["stack"][h][p // 2].wait(pe, st, 0)
                            n = SHIFT + 1
                            mm = pe.matmul(ps[0:PR, bank, 0:KB], qst[0:n, nb, rows], kst[0:n, nb, p // 2, ks],
                                           start=True, stop=True)
                    else:
                        L["prep"].wait(pe, st, prep_count(l, st, "R"))
                        mm = pe.matmul(ps[SHIFT:SHIFT + NSH, bank, 0:PR], mx[:, 0:NSH], negid[:], start=True, stop=True)
                    mm.then_inc(L["filled"].sem, 1)

                def body(st, par, main, prep):
                    i = 0
                    def units(c, part):
                        nonlocal i
                        names = plan(l, st)[c]
                        cut = len(names) // 2
                        for name in (names[:cut], names[cut:])[part]:
                            unit(st, par, name, i)
                            i += 1

                    for c in range(CH):
                        first = UNITS_FIRST[l] and c == 0
                        if prep and first:
                            units(c, 0)
                            units(c, 1)
                        if main:
                            scores(st, par, c)
                        if prep and not first:
                            units(c, 0)
                        if main:
                            for v in PV_AT[l][c]:
                                if v >= 0:
                                    values(st, par, v, 0)
                                elif st.j is not None or st.c > 0:
                                    values(st, 1 - par, CH + v, 1)
                            if c == OUT_AT and (st.j is not None or st.c > 0):
                                turn_out(st, 1)
                        if prep and not first:
                            units(c, 1)
                    if main and not prep:
                        for c in (CH - 2, CH - 1):
                            values(st, par, c, 0)
                        turn_out(st, 0)

                steps(pe, body, l)

            def experts(l):
                M = moe[l]
                if l == 0:
                    pe.wait_ge(setup, N_SETUP)
                for i in range(NT):
                    o = ps[:, 7, E * i:E * i + E]
                    ts = slice(128 * i, 128 * i + 128)
                    pe.matmul(o, xTh[:, ts], wrh[l][:], start=True, stop=False)
                    pe.matmul(o, xTh[:, ts], wrl[l][:], start=False, stop=False)
                    mm = pe.matmul(o, xTl[:, ts], wrh[l][:], start=False, stop=True)
                mm.then_inc(M["lg"], 1)

                def routing():
                    pe.wait_ge(M["ch"], 1)
                    if l == 0:
                        pe.transpose(ps[0:NT * E, 7, 0:128], gate[:].rearrange("p i e -> p (i e)"), ident[:]).then_inc(M["rp"], 1)
                        pe.wait_ge(M["gt"], 1)
                        return
                    for k in range(2):
                        oh = rt[:, 4 + k].rearrange("p i e -> p (i e)")
                        pe.matmul(ps[:, 7, 256 * k:256 * k + NT * E], tri[:], oh, start=True, stop=True)
                        mm = pe.matmul(ps[:, 7, 256 * k + 128:256 * k + 128 + NT * E], real[:], oh, start=True, stop=True)
                    mm.then_inc(M["rp"], 1)

                def biases(g):
                    if g > 1:
                        pe.wait_ge(M["rd"], g - 1)
                    for t in range(4):
                        i = 4 * g + t
                        mm = pe.matmul(ps[:, 6 + g % 2, 128 * t:128 * t + 128], gateT[0:NT * E, :], b2x[0:NT * E, i, :],
                                       start=True, stop=True)
                    mm.then_inc(M["rp"], 1)

                def up(e, par, g):
                    for f in range(NF):
                        n = g * NF + f
                        if n > 3 or not (isinstance(e, int) and e == 0):
                            pe.wait_ge(M["act"], e * (G * NF) + (n - 3))
                        xh, xl = [t[:, 512 * g:512 * g + 512].rearrange("p (b s) -> p b s", s=PB)[:, :, 0:S] for t in (xTh, xTl)]
                        o = ps[:, n % 4, 0:8 * S].rearrange("p (b s) -> p b s", s=S)
                        fs = slice(128 * f, 128 * f + 128)
                        pe.matmul(o, uph[:, par, fs], xh, start=True, stop=False)
                        pe.matmul(o, uph[:, par, fs], xl, start=False, stop=False)
                        pe.matmul(o, upl[:, par, fs], xh, start=False, stop=True).then_inc(M["up"], 1)

                def down(e, par, q):
                    pe.wait_ge(M["lo"], e * (G * NF) + NF * (q + 1))
                    if q > 1 or not (isinstance(e, int) and e == 0):
                        pe.wait_ge(M["add"], e * G + (q - 1))
                    for t in range(4):
                        for f in range(NF):
                            o = ps[:, 4 + q % 2, 128 * t:128 * t + 128]
                            hh, hl = [h[:, q % 2, f, 2 * t:2 * t + 2, :].rearrange("p b s -> p (b s)") for h in (hTh, hTl)]
                            pe.matmul(o, hh, dnh[:, par, f, :], start=(f == 0), stop=False)
                            pe.matmul(o, hh, dnl[:, par, f, :], start=False, stop=False)
                            mm = pe.matmul(o, hl, dnh[:, par, f, :], start=False, stop=(f == NF - 1))
                    mm.then_inc(M["dn"], 1)

                def expert(e, par):
                    first = isinstance(e, int) and e == 0
                    pe.wait_ge(M["sp"], e * 6 + 6)
                    for g in range(G):
                        up(e, par, g)
                        if g > 0:
                            down(e, par, g - 1)
                        elif not first:
                            down(e - 1, 1 - par, G - 1)
                        if first and g == 1:
                            routing()
                        if first and l == 0 and g > 0:
                            for i in range(2) if g == 1 else (g,):
                                biases(i)

                expert(0, 0)
                expert(1, 1)
                with pe.Fori(1, E // 2) as j:
                    expert(j * 2, 0)
                    expert(j * 2 + 1, 1)
                down(E - 1, 1, G - 1)

            transpose_tokens(0)
            attention(0)
            transpose_tokens(1)
            experts(0)
            transpose_tokens(2)
            attention(1)
            transpose_tokens(3)
            experts(1)

        @block.vector
        def _(dve):
            NX = (NT + 3) // 4
            dve.wait_ge(loaded[0], N_LOADED)
            dve.wait_ge(setup, N_SETUP0)
            lns = [0]

            def link(ins):
                lns[0] += 1
                ins.then_inc(ln_step, 1)
                dve.wait_ge(ln_step, lns[0])

            for w, hi, lo in ((wv_s[0], wvh[0], wvl[0]), (wv_s[1], wvh[1], wvl[1]), (wk1_s, wk1h, wk1l)):
                link(dve.tensor_copy(hi[:], w[:]))
                link(dve.tensor_tensor(lo[:], w[:], hi[:], ALU.subtract))
            for l in range(2):
                link(dve.tensor_scalar(wr_s[l][:], wr_s[l][:], WS, None, ALU.mult))
                link(dve.tensor_copy(wrh[l][:], wr_s[l][:]))
                link(dve.tensor_tensor(wrl[l][:], wr_s[l][:], wrh[l][:], ALU.subtract))
            rs = float(1.0 / np.sqrt(np.float32(W)))
            for r in range(3):
                link(dve.tensor_scalar(wq1r[:, :, r, :], wq1_s[:].rearrange("p (g w) -> p g w", g=NG), rs, None, ALU.mult))
            link(dve.tensor_scalar(bqs[:], bqr_s[:], rs, None, ALU.mult))
            dve.tensor_scalar(mf[:], mi[:], -1.0, None, ALU.add).then_inc(mf_kept, 1)
            for n in range(4):
                dve.wait_ge(g_ready, n + 1)
                gs = slice(4 * D * n, 4 * D * n + 4 * D)
                link(dve.tensor_scalar(gh[:, gs], ps[:, n, :], WS * float(DK0) ** -0.5, None, ALU.mult))
                dve.scalar_tensor_tensor(out=gl[:, gs], in0=ps[:, n, :], scalar=WS * float(DK0) ** -0.5, in1=gh[:, gs],
                                         op0=ALU.mult, op1=ALU.subtract).then_inc(g_kept, 1)
            link(dve.tensor_tensor(b2x[:], b2_s[:].unsqueeze(1).broadcast_to([128, NT, D]),
                                   selte[:].unsqueeze(2).broadcast_to([128, NT, D]), ALU.mult))

            def norm(n):
                link(dve.tensor_reduce(stat[:, 0, :], xs[:], AX.X, ALU.add))
                link(dve.tensor_scalar(stat[:, 1, :], stat[:, 0, :], 1.0 / D, None, ALU.mult))
                link(dve.tensor_tensor(xc[:], xs[:], stat[:, 1, :].unsqueeze(2).broadcast_to([128, NT, D]), ALU.subtract))
                link(dve.tensor_tensor(xsq[:], xc[:], xc[:], ALU.mult))
                link(dve.tensor_reduce(stat[:, 0, :], xsq[:], AX.X, ALU.add))
                dve.tensor_scalar(stat[:, 2, :], stat[:, 0, :], 1.0 / D, EPS, ALU.mult, ALU.add).then_inc(ln_var, 1)
                dve.wait_ge(ln_std, n + 1)
                link(dve.reciprocal(stat[:, 4, :], stat[:, 3, :]))
                link(dve.tensor_tensor(stat[:, 5, :], stat[:, 4, :], stat[:, 4, :], ALU.mult))
                link(dve.tensor_tensor(stat[:, 5, :], stat[:, 5, :], stat[:, 2, :], ALU.mult))
                link(dve.tensor_scalar(stat[:, 5, :], stat[:, 5, :], -0.5, 1.5, ALU.mult, ALU.add))
                link(dve.tensor_tensor(stat[:, 4, :], stat[:, 4, :], stat[:, 5, :], ALU.mult))
                dve.tensor_tensor(xc[:], xc[:], stat[:, 4, :].unsqueeze(2).broadcast_to([128, NT, D]),
                                  ALU.mult).then_inc(ln_xn, 1)
                for i in range(G):
                    dve.wait_ge(xT_kept, n * G + i + 1)
                    dve.wait_ge(xh_kept, n * G + i + 1)
                    ts = slice(512 * i, 512 * i + 512)
                    ins = dve.tensor_tensor(xTl[:, ts], xT[:, ts], xTh[:, ts], ALU.subtract)
                ins.then_inc(xl_kept, 1)

            def split(l, e, par):
                M = moe[l]
                dve.wait_ge(M["wl"][par], 32 if isinstance(e, int) and e < 2 else e * 16 + (32 - 16 * par))
                for k, (w, hi, lo) in enumerate(((up_s, uph, upl), (down_s, dnh, dnl))):
                    w, hi, lo = [t[:, par] if len(t.shape) == 3 else t[:, par].rearrange("p f d -> p (f d)") for t in (w, hi, lo)]
                    dve.tensor_scalar(w, w, WS, None, ALU.mult).then_inc(M["sp"], 1)
                    dve.wait_ge(M["sp"], e * 6 + (3 * k + 1))
                    dve.tensor_copy(hi, w).then_inc(M["sp"], 1)
                    dve.wait_ge(M["sp"], e * 6 + (3 * k + 2))
                    dve.tensor_tensor(lo, w, hi, ALU.subtract).then_inc(M["sp"], 1)

            def attention(l):
                L = lay[l]

                def keep_sums(st, back):
                    L["pv"].wait(dve, st, CH, back=back)
                    dve.tensor_copy(o_s[:].rearrange("p s n -> p (s n)"), ps[:, 7, 0:2 * PR]).then_inc(L["o_kept"].sem, 1)

                def add_out(st, back):
                    base = PB * ((st.c - back) % 2)
                    rows = slice(base, base + S)
                    O = L["out"]
                    L["outT"].wait(dve, st, 1, back=back)
                    src = ps[rows, 7, :].rearrange("p (s a j w) -> p s a j w", s=2, a=2, j=NG)
                    dve.reciprocal(rden[rows], src[:, :, :, :, 2 * W]).then_inc(O.sem, 1)
                    O.wait(dve, st, 1, back=back)
                    dst = on[rows, :].rearrange("p (s j a w) -> p s a j w", s=2, j=NG, a=2)
                    for a in range(2):
                        dve.tensor_tensor(dst[:, :, a], src[:, :, a, :, W * a:W * a + W],
                                          rden[rows, :, a, :].unsqueeze(3).broadcast_to([S, 2, NG, W]),
                                          ALU.mult).then_inc(O.sem, 1)
                    k = 3
                    O.wait(dve, st, k, back=back)
                    if l == 1:
                        dve.tensor_tensor(on[rows], on[rows], bv_s[rows], ALU.add).then_inc(O.sem, 1)
                        k += 1
                        O.wait(dve, st, k, back=back)
                    ti = tile_index(st, -back)
                    xv = xs[rows, ti, :] if isinstance(ti, int) else xs[rows, bass.ds(ti, 1), :].squeeze(1)
                    dve.tensor_tensor(xv, xv, on[rows, :], ALU.add).then_inc(O.sem, 1)

                def unit(st, nb, name, i, highs):
                    F, P = L["free"], L["prep"]
                    if name[0] in ACT_RELEASES[l]:
                        return
                    L["filled"].wait(dve, st, i + 1)
                    bank = bank_of(l, st, i)
                    k = int(name[1:] or 0)
                    if name[0] == "T":
                        ks = slice(KB * k, KB * k + KB)
                        L["high"].wait(dve, st, highs)
                        dve.tensor_tensor(cTl[:, nb, ks], ps[:, bank, 0:KB], cTh[:, nb, ks], ALU.subtract).then_inc(F.sem, 1)
                    elif name[0] == "Q" and l == 0:
                        cs = slice(HB * k, HB * k + HB)
                        L["high"].wait(dve, st, highs)
                        dve.scalar_tensor_tensor(out=ql[:, nb, cs], in0=ps[:, bank, 0:HB], scalar=1.0 / WS, in1=qh[:, nb, cs],
                                                 op0=ALU.mult, op1=ALU.subtract).then_inc(F.sem, 1)
                    elif name[0] == "Q":
                        dve.tensor_tensor(qt[:], ps[0:SHIFT, bank, 0:NG * S].rearrange("p (g s) -> p g s", g=NG),
                                          bqs[:].unsqueeze(2).broadcast_to([SHIFT, NG, S]), ALU.add).then_inc(F.sem, 1)
                        wait_read(dve, l, st, i)
                        L["spread"].wait(dve, st, 1)
                        dve.tensor_copy(qhl[:], qt[:]).then_inc(P.sem, 1)
                        P.wait(dve, st, prep_count(l, st, name) + 1)
                        dve.tensor_tensor(qhl[2 * GW:], qt[2 * GW:], qhl[2 * GW:], ALU.subtract).then_inc(P.sem, 1)
                    elif name[0] == "M":
                        p, kb = max_unit(l, k)
                        dve.tensor_reduce(mp[:, p, kb:kb + 1], ps[0:PR, bank, 0:KB], AX.X, ALU.max).then_inc(F.sem, 1)
                        if k == 3 * NP - 1:
                            wait_read(dve, l, st, i)
                            dve.tensor_reduce(mx[:, 1:NSH], mp[:], AX.X, ALU.max).then_inc(P.sem, 1)
                    else:
                        dst = sh[SHIFT:SHIFT + NSH, nb, :] if l == 0 else qst[SHIFT:SHIFT + NSH, nb, :]
                        dve.tensor_tensor(dst.rearrange("p (q n) -> p q n", q=NP),
                                          ps[SHIFT:SHIFT + NSH, bank, 0:PR].unsqueeze(1).broadcast_to([NSH, NP, PR]),
                                          sel[l][SHIFT:SHIFT + NSH, :].unsqueeze(2).broadcast_to([NSH, NP, PR]),
                                          ALU.mult).then_inc(F.sem, 1)

                def body(st, par, main, prep):
                    i = highs = 0
                    for c in range(CH):
                        if main and (st.j is not None or st.c > 0):
                            if c == 2:
                                keep_sums(st, 1)
                            if c == OUT_AT + 1:
                                add_out(st, 1)
                        if prep:
                            for name in plan(l, st)[c]:
                                highs += name[0] in ACT_READS[l]
                                unit(st, batch_of(l, par, name)[1], name, i, highs)
                                i += 1
                    if main and not prep:
                        if l == 0:
                            wait_read(dve, 0, st, "Q1", back=1)
                        split(l, 0, 0)
                        split(l, 1, 1)
                        keep_sums(st, 0)
                        add_out(st, 0)
                        L["out"].wait(dve, st, L["out"].per)

                steps(dve, body, l)

            def experts(l):
                M = moe[l]
                if l == 0:
                    dve.wait_ge(setup, N_SETUP)
                n = [0]

                def link(ins):
                    n[0] += 1
                    ins.then_inc(M["rs"], 1)
                    dve.wait_ge(M["rs"], n[0])

                def wide(a):
                    return a.unsqueeze(2).broadcast_to([128, NT, E])

                ev = eidx[:].unsqueeze(1).broadcast_to([128, NT, E])

                def first_of(dst, values, scratch, m):
                    link(dve.tensor_reduce(m, values, AX.X, ALU.max))
                    link(dve.tensor_tensor(scratch, values, wide(m), ALU.is_equal))
                    link(dve.tensor_tensor(scratch, scratch, ev, ALU.mult))
                    link(dve.tensor_reduce(m, scratch, AX.X, ALU.max))
                    link(dve.tensor_tensor(dst, scratch, wide(m), ALU.is_equal))

                lg = ps[:, 7, 0:NT * E].rearrange("p (i e) -> p i e", e=E)
                dve.wait_ge(M["lg"], 1)
                link(dve.tensor_scalar(rt[:, 0], lg, 1.0 / WS, None, ALU.mult))
                link(dve.tensor_reduce(r1[:, 0], rt[:, 0], AX.X, ALU.max))
                dve.tensor_tensor(rt[:, 1], rt[:, 0], wide(r1[:, 0]), ALU.subtract).then_inc(M["lm"], 1)
                dve.wait_ge(M["ex"], 1)
                if l == 0:
                    first_of(rt[:, 4], rt[:, 2], rt[:, 3], r1[:, 1])
                    link(dve.tensor_reduce(r1[:, 2], rt[:, 2], AX.X, ALU.add))
                    link(dve.tensor_reduce(r1[:, 4], rt[:, 2], AX.X, ALU.max))
                    link(dve.reciprocal(r1[:, 3], r1[:, 2]))
                    link(dve.tensor_tensor(r1[:, 3], r1[:, 3], r1[:, 4], ALU.mult))
                    dve.tensor_tensor(gate[:], rt[:, 4], wide(r1[:, 3]), ALU.mult).then_inc(M["ch"], 1)
                    dve.wait_ge(M["rp"], 1)
                    dve.tensor_copy(gateT[0:NT * E, :], ps[0:NT * E, 7, 0:128]).then_inc(M["gt"], 1)
                else:
                    first_of(rt[:, 4], rt[:, 1], rt[:, 3], r1[:, 1])
                    link(dve.scalar_tensor_tensor(out=rt[:, 6], in0=rt[:, 4], scalar=-3.0e38, in1=rt[:, 1],
                                                  op0=ALU.mult, op1=ALU.add))
                    first_of(rt[:, 5], rt[:, 6], rt[:, 3], r1[:, 2])
                    link(dve.tensor_tensor(rt[:, 8], rt[:, 2], rt[:, 5], ALU.mult))
                    link(dve.tensor_reduce(r1[:, 4], rt[:, 8], AX.X, ALU.add))
                    link(dve.tensor_scalar(r1[:, 5], r1[:, 4], 1.0, None, ALU.add))
                    link(dve.reciprocal(r1[:, 6], r1[:, 5]))
                    dve.tensor_tensor(r1[:, 7], r1[:, 4], r1[:, 6], ALU.mult).then_inc(M["ch"], 1)
                    dve.wait_ge(M["rp"], 1)
                    for k in range(2):
                        pre = ps[:, 7, 256 * k:256 * k + NT * E].rearrange("p (i e) -> p i e", e=E)
                        tot = ps[:, 7, 256 * k + 128:256 * k + 128 + NT * E].rearrange("p (i e) -> p i e", e=E)
                        a, b = 8, 9
                        link(dve.tensor_copy(rt[:, a], tot))
                        d = 1
                        while d < NT:
                            link(dve.tensor_copy(rt[:, b, 0:d], rt[:, a, 0:d]))
                            link(dve.tensor_tensor(rt[:, b, d:NT], rt[:, a, d:NT], rt[:, a, 0:NT - d], ALU.add))
                            a, b, d = b, a, 2 * d
                        if k == 0:
                            link(dve.tensor_copy(rt[:, 12, 0:1], rt[:, a, NT - 1:NT]))
                        link(dve.tensor_tensor(rt[:, 10], rt[:, a], tot, ALU.subtract))
                        link(dve.tensor_tensor(rt[:, 10], rt[:, 10], pre, ALU.add))
                        if k == 1:
                            link(dve.tensor_tensor(rt[:, 10], rt[:, 10], rt[:, 12, 0:1, :].broadcast_to([128, NT, E]), ALU.add))
                        link(dve.scalar_tensor_tensor(out=rt[:, 11], in0=rt[:, 10], scalar=float(cap), in1=rt[:, 4 + k],
                                                      op0=ALU.is_lt, op1=ALU.mult))
                        link(dve.tensor_tensor(rt[:, 13 + k], rt[:, 11], wide(r1[:, 6 + k]), ALU.mult))
                    link(dve.tensor_tensor(gate[:], rt[:, 13], rt[:, 14], ALU.add))
                link(dve.tensor_scalar(gate_s[:], gate[:], 1.0 / WS, None, ALU.mult))

                def biases(g):
                    dve.wait_ge(M["rp"], 2 + g)
                    xv = xs[:, 4 * g:4 * g + 4, :]
                    dve.tensor_tensor(xv, xv, ps[:, 6 + g % 2, :].rearrange("p (t d) -> p t d", d=D), ALU.add).then_inc(M["rd"], 1)

                def add(e, g):
                    dve.wait_ge(M["dn"], e * G + (g + 1))
                    if not (isinstance(e, int) and e == 0):
                        dve.wait_ge(M["add"], e * G + (g + 1 - G))
                    elif l == 0:
                        dve.wait_ge(M["rd"], g + 1)
                    bank = 4 + g % 2
                    for t in range(4):
                        i = 4 * g + t
                        ins = dve.scalar_tensor_tensor(out=xs[:, i, :], in0=ps[:, bank, 128 * t:128 * t + 128],
                                                       scalar=gate_s[:, i, e:e + 1] if isinstance(e, int) else gate_s[:, i, bass.ds(e, 1)],
                                                       in1=xs[:, i, :], op0=ALU.mult, op1=ALU.add)
                    ins.then_inc(M["add"], 1)

                def expert(e, par, more=True):
                    first = isinstance(e, int) and e == 0
                    if not first:
                        add(e - 1, G - 1)
                        if more:
                            split(l, e + 1, 1 - par)
                    for g in range(1, G):
                        if first and l == 0:
                            for i in range(2) if g == 1 else (g,):
                                biases(i)
                        add(e, g - 1)

                expert(0, 0)
                expert(1, 1)
                with dve.Fori(1, E // 2 - 1) as j:
                    expert(j * 2, 0)
                    expert(j * 2 + 1, 1)
                expert(E - 2, 0)
                expert(E - 1, 1, more=False)
                add(E - 1, G - 1)
                dve.wait_ge(M["add"], E * G)

            norm(0)
            attention(0)
            norm(1)
            experts(0)
            norm(2)
            attention(1)
            norm(3)
            experts(1)



_IN = ["x", "ctx", "mask", "wqT", "wkT", "wv", "wr0", "w1", "b1", "w2", "b2rep", "wq1T", "bqr", "wk1T", "bk", "wv1T", "bv",
       "wg", "fc", "proj", "ident", "negid", "hmask", "sel0", "sel1", "selte", "tri", "real", "eidx"]


def constants(NT):
    p = np.arange(128)
    is_real = (p % PB) < S
    sel1 = np.zeros((128, NP), np.float32)
    for t in range(NP):
        sel1[SHIFT + 1 + t, t] = 1
    sel0 = sel1.copy()
    sel1[SHIFT] = 1
    return dict(
        ident=np.eye(128, dtype=np.float32), negid=-np.eye(PR, dtype=np.float32),
        hmask=((p[:SHIFT, None] % GW) // W == np.arange(4)).astype(np.float16), sel0=sel0, sel1=sel1,
        selte=(p[:, None] // E == np.arange(NT)).astype(np.float32),
        tri=((p[:, None] < p[None]) & is_real[:, None]).astype(np.float32),
        real=np.repeat(is_real[:, None], 128, 1).astype(np.float32),
        eidx=np.repeat((E - np.arange(E, dtype=np.float32))[None], 128, 0))


def laid_out(i):
    a = {k: np.asarray(v) for k, v in i.items()}
    B = a["x"].shape[0]
    NT = B // 2
    d = dict(
        x=a["x"], ctx=a["ctx_1024"], mask=a["mask_BxS2_ik0"], wqT=a["L0_xattn_wq"].T, wkT=a["L0_xattn_wk"].T,
        wv=a["L0_xattn_wv"], wr0=a["L0_ffn_Wr"], w1=a["L0_ffn_W1"],
        b1=a["L0_ffn_b1"].reshape(E, NF, 128).transpose(2, 0, 1),
        w2=a["L0_ffn_W2"].reshape(E, NF, 128, D).transpose(0, 2, 1, 3), b2rep=np.tile(a["L0_ffn_b2"], (128 // E, 1)),
        wq1T=a["L1_xattn_Wq"].T, bqr=np.tile(a["L1_xattn_bq"].reshape(NG, GW).T, (3, 1)), wk1T=a["L1_xattn_Wk"].T,
        bk=a["L1_xattn_bk"].reshape(D, 1), wv1T=a["L1_xattn_Wv"].T, bv=np.tile(a["L1_xattn_bv"][None], (S + PB, 1)),
        wg=a["L1_ffn_w_g"], fc=a["L1_ffn_c_fc"], proj=a["L1_ffn_c_proj"].reshape(E, NF, 128, D).transpose(0, 2, 1, 3))
    d.update(constants(NT))
    return B, {k: np.ascontiguousarray(v) for k, v in d.items()}


def kernel(**inputs):
    import concourse.bacc as bacc
    from concourse.bass_utils import run_bass_kernel_spmd

    B, arrays = laid_out(inputs)
    nc = bacc.Bacc("TRN2", target_bir_lowering=False, num_devices=1)
    arrays = {"in_" + n: a for n, a in arrays.items()}
    args = [nc.dram_tensor(n, arrays[n].shape, mybir.dt.from_np(arrays[n].dtype), kind="ExternalInput").ap() for n in ("in_" + n for n in _IN)]
    out = nc.dram_tensor("out", [B, S, D], F32, kind="ExternalOutput").ap()
    program(nc, B, args, out)
    r = run_bass_kernel_spmd(nc, [arrays], core_ids=[0])
    return r.results[0]["out"]
```
